# Optimizing a Trainium2 kernel written in Bass

```python
import numpy as np
import jax
import jax.numpy as jnp

def _softmax(x, axis=-1):
    return jax.nn.softmax(x, axis=axis)

def _gelu(x):
    return jax.nn.gelu(x, approximate=True)

def _silu(x):
    return jax.nn.silu(x)

def _sigmoid(x):
    return jax.nn.sigmoid(x)

def _layernorm(x, axis=-1, eps=1e-05):
    m = jnp.mean(x, axis=axis, keepdims=True)
    v = jnp.var(x, axis=axis, keepdims=True)
    return (x - m) / jnp.sqrt(v + eps)

def _scatter_add(tgt, idx, src, axis=0):
    return tgt.at[idx].add(src)

def _segment_sum(src, seg, n):
    return jax.ops.segment_sum(src, seg, n)
kernel_name = 'mk_vit_tower_cls_d2_tok_img256_r4_68784e'

def setup_inputs(seed: int=0):
    np.random.seed(seed)
    _w = jnp.asarray

    def _rec_inputs():
        import jax
        import jax.numpy as jnp
        _rk = jax.random.key(seed)
        x = -7.10856e-05 + 0.999911 * jax.random.normal(jax.random.fold_in(_rk, 1), (128, 1, 96, 96), jnp.float32)
        cls_tok = 0.02 * jax.random.normal(jax.random.fold_in(_rk, 5), (1, 1, 64), jnp.float32)
        return (x, cls_tok)
    x, cls_tok = _rec_inputs()

    def _L0_tok_setup():
        import jax, jax.numpy as jnp
        import numpy as np
        INV_SQRT2 = 0.7071067811865476

        def haar_dwt2(x):
            lo = (x[..., ::2] + x[..., 1::2]) * INV_SQRT2
            hi = (x[..., ::2] - x[..., 1::2]) * INV_SQRT2
            cA = (lo[..., ::2, :] + lo[..., 1::2, :]) * INV_SQRT2
            cH = (lo[..., ::2, :] - lo[..., 1::2, :]) * INV_SQRT2
            cV = (hi[..., ::2, :] + hi[..., 1::2, :]) * INV_SQRT2
            cD = (hi[..., ::2, :] - hi[..., 1::2, :]) * INV_SQRT2
            return (cA, (cH, cV, cD))

        def wavedec2_maps(x, levels):
            a = x
            details = []
            for _ in range(levels):
                a, d = haar_dwt2(a)
                details.append(d)
            maps = [a]
            for d in reversed(details):
                maps.extend(d)
            return maps
        key = jax.random.key(seed)
        k1, k2 = jax.random.split(key)
        B, H, W_img = (64, 256, 256)
        x = jax.random.normal(k1, (B, 1, H, W_img), dtype=jnp.float32)
        n_maps = 1 + 3 * 2
        W = jax.random.normal(k2, (n_maps, 64), dtype=jnp.float32) * (1.0 / np.sqrt(n_maps))
        b = jnp.zeros((64,), dtype=jnp.float32)
        return {'x': x, 'W': W, 'b': b}
    _L0_tok_all = _L0_tok_setup()
    _L0_tok_in = {k: v for k, v in _L0_tok_all.items() if k in ('W', 'b')}
    del _L0_tok_all

    def _L0_attn_setup():
        import jax, jax.numpy as jnp
        import numpy as np
        import math
        D = 64
        K = 32
        B = 2
        L = 512
        MAX_SEQ = 2048
        PI = math.pi

        def _content_stream(x, Wk1, bk1, Wk2, bk2, Wq1, bq1, Wq2, bq2, Wvc, bvc):
            Bc, Lc, Dc = x.shape
            key_phase = jnp.tanh(jnp.tanh(x @ Wk1 + bk1) @ Wk2 + bk2) * PI
            query_phase = jnp.tanh(jnp.tanh(x @ Wq1 + bq1) @ Wq2 + bq2) * PI
            value = x @ Wvc + bvc
            cos_k = jnp.cos(key_phase)[..., None]
            sin_k = jnp.sin(key_phase)[..., None]
            v_e = value[:, :, None, :]
            mem_real = jnp.cumsum(cos_k * v_e, axis=1)
            mem_imag = jnp.cumsum(sin_k * v_e, axis=1)
            cos_q = jnp.cos(query_phase)[..., None]
            sin_q = jnp.sin(query_phase)[..., None]
            retrieved = (mem_real * cos_q + mem_imag * sin_q).sum(axis=2)
            positions = jnp.arange(1, Lc + 1, dtype=jnp.float32)
            norm = jnp.sqrt(positions * K)[None, :, None]
            return retrieved / norm

        def _pos_stream(x, base_phases, Wvp, bvp):
            Bc, Lc, Dc = x.shape
            phases = base_phases[:Lc][None]
            value = x @ Wvp + bvp
            cos_p = jnp.cos(phases)
            sin_p = jnp.sin(phases)
            mem_real = jnp.cumsum(value * cos_p, axis=1)
            mem_imag = jnp.cumsum(value * sin_p, axis=1)
            retrieved = mem_real * cos_p + mem_imag * sin_p
            positions = jnp.arange(1, Lc + 1, dtype=jnp.float32)
            return retrieved / jnp.sqrt(positions)[None, :, None]
        key = jax.random.key(seed)
        ks = jax.random.split(key, 24)
        s = 0.02
        inp = {}
        inp['x'] = jax.random.normal(ks[0], (B, L, D), dtype=jnp.float32)
        inp['base_phases'] = jax.random.normal(ks[1], (MAX_SEQ, D), dtype=jnp.float32) * PI
        inp['Wk1'] = jax.random.normal(ks[2], (D, D), dtype=jnp.float32) * s
        inp['bk1'] = jnp.zeros((D,), jnp.float32)
        inp['Wk2'] = jax.random.normal(ks[3], (D, K), dtype=jnp.float32) * s
        inp['bk2'] = jnp.zeros((K,), jnp.float32)
        inp['Wq1'] = jax.random.normal(ks[4], (D, D), dtype=jnp.float32) * s
        inp['bq1'] = jnp.zeros((D,), jnp.float32)
        inp['Wq2'] = jax.random.normal(ks[5], (D, K), dtype=jnp.float32) * s
        inp['bq2'] = jnp.zeros((K,), jnp.float32)
        inp['Wvc'] = jax.random.normal(ks[6], (D, D), dtype=jnp.float32) * s
        inp['bvc'] = jnp.zeros((D,), jnp.float32)
        inp['Wvp'] = jax.random.normal(ks[7], (D, D), dtype=jnp.float32) * s
        inp['bvp'] = jnp.zeros((D,), jnp.float32)
        inp['Wg1'] = jax.random.normal(ks[8], (D, D // 4), dtype=jnp.float32) * s
        inp['bg1'] = jnp.zeros((D // 4,), jnp.float32)
        inp['Wg2'] = jax.random.normal(ks[9], (D // 4, 2), dtype=jnp.float32) * s
        inp['bg2'] = jnp.zeros((2,), jnp.float32)
        inp['ln_g'] = jnp.ones((D,), jnp.float32)
        inp['ln_b'] = jnp.zeros((D,), jnp.float32)
        inp['Wo'] = jax.random.normal(ks[10], (D, D), dtype=jnp.float32) * s
        inp['bo'] = jnp.zeros((D,), jnp.float32)
        return inp
    _L0_attn_all = _L0_attn_setup()
    _L0_attn_in = {k: v for k, v in _L0_attn_all.items() if k in ('base_phases', 'Wk1', 'bk1', 'Wk2', 'bk2', 'Wq1', 'bq1', 'Wq2', 'bq2', 'Wvc', 'bvc', 'Wvp', 'bvp', 'Wg1', 'bg1', 'Wg2', 'bg2', 'ln_g', 'ln_b', 'Wo', 'bo')}
    del _L0_attn_all

    def _L0_ffn_setup():
        import jax, jax.numpy as jnp
        import numpy as np
        B, S, D, H, E, K = (8, 2048, 64, 256, 8, 2)
        key = jax.random.key(seed)
        ks = jax.random.split(key, 7)
        s_in = 1.0 / np.sqrt(D)
        s_hid = 1.0 / np.sqrt(H)
        return {'x': jax.random.normal(ks[0], (B, S, D), dtype=jnp.float32), 'Wg': jax.random.uniform(ks[1], (E, D), jnp.float32, -s_in, s_in), 'bg': jax.random.uniform(ks[2], (E,), jnp.float32, -s_in, s_in), 'W1': jax.random.uniform(ks[3], (E, H, D), jnp.float32, -s_in, s_in), 'b1': jax.random.uniform(ks[4], (E, H), jnp.float32, -s_in, s_in), 'W2': jax.random.uniform(ks[5], (E, D, H), jnp.float32, -s_hid, s_hid), 'b2': jax.random.uniform(ks[6], (E, D), jnp.float32, -s_hid, s_hid)}
    _L0_ffn_all = _L0_ffn_setup()
    _L0_ffn_in = {k: v for k, v in _L0_ffn_all.items() if k in ('Wg', 'bg', 'W1', 'b1', 'W2', 'b2')}
    del _L0_ffn_all

    def _L1_attn_setup():
        import jax, jax.numpy as jnp
        import numpy as np
        import math
        STATE_DIM = 64
        R_MIN, R_MAX = (0.4, 0.9)
        PHASE_MAX = 2.0 * math.pi
        BATCH, SEQ = (8, 1024)

        def _binop(e_i, e_j):
            a_i, b_i = e_i
            a_j, b_j = e_j
            return (a_j * a_i, a_j * b_i + b_j)
        key = jax.random.key(seed)
        k_x, k_u1, k_u2, k_br, k_bi, k_cr, k_ci = jax.random.split(key, 7)
        D = STATE_DIM
        x = jax.random.normal(k_x, (BATCH, SEQ, D), dtype=jnp.float32)
        u1 = jax.random.uniform(k_u1, (D,), dtype=jnp.float32)
        nu_log = jnp.log(-0.5 * jnp.log(u1 * (R_MAX + R_MIN) * (R_MAX - R_MIN) + R_MIN ** 2))
        u2 = jax.random.uniform(k_u2, (D,), dtype=jnp.float32)
        theta_log = jnp.log(PHASE_MAX * u2)
        lam_mod = jnp.exp(-jnp.exp(nu_log))
        gamma_log = jnp.log(jnp.sqrt(1.0 - jnp.square(lam_mod)))
        s_b = 1.0 / math.sqrt(2 * D)
        s_c = 1.0 / math.sqrt(D)
        B_re = jax.random.normal(k_br, (D, D), dtype=jnp.float32) * s_b
        B_im = jax.random.normal(k_bi, (D, D), dtype=jnp.float32) * s_b
        C_re = jax.random.normal(k_cr, (D, D), dtype=jnp.float32) * s_c
        C_im = jax.random.normal(k_ci, (D, D), dtype=jnp.float32) * s_c
        return {'x': x, 'nu_log': nu_log, 'theta_log': theta_log, 'gamma_log': gamma_log, 'B_re': B_re, 'B_im': B_im, 'C_re': C_re, 'C_im': C_im}
    _L1_attn_all = _L1_attn_setup()
    _L1_attn_in = {k: v for k, v in _L1_attn_all.items() if k in ('nu_log', 'theta_log', 'gamma_log', 'B_re', 'B_im', 'C_re', 'C_im')}
    del _L1_attn_all

    def _L1_ffn_setup():
        import jax, jax.numpy as jnp
        import numpy as np
        B, T, C = (64, 96, 64)
        NH, NKV = (4, 2)
        HD = C // NH
        NREP = NH // NKV
        NE, TOPK = (8, 2)
        HID = int(8 / 3 * C)
        EPS_RMS = 1e-06

        def _rope_tables(t_len):
            inv_freq = 1.0 / 10000.0 ** (np.arange(0, HD, 2, dtype=np.float32) / HD)
            t = np.arange(t_len, dtype=np.float32)
            freqs = np.outer(t, inv_freq)
            emb = np.concatenate([freqs, freqs], axis=-1)
            return (jnp.asarray(np.cos(emb)), jnp.asarray(np.sin(emb)))

        def _rotate_half(x):
            h = x.shape[-1] // 2
            return jnp.concatenate([-x[..., h:], x[..., :h]], axis=-1)

        def _rmsnorm(v, w):
            return v * jax.lax.rsqrt(jnp.mean(v * v, axis=-1, keepdims=True) + EPS_RMS) * w
        key = jax.random.key(seed)
        ks = jax.random.split(key, 10)
        s = lambda k, shape: jax.random.normal(k, shape, jnp.float32) * 0.02
        return {'x': jax.random.normal(ks[0], (B, T, C), jnp.float32), 'ln1_w': jnp.ones((C,), jnp.float32), 'ln2_w': jnp.ones((C,), jnp.float32), 'wq': s(ks[1], (NH * HD, C)), 'wk': s(ks[2], (NKV * HD, C)), 'wv': s(ks[3], (NKV * HD, C)), 'wo': s(ks[4], (C, C)), 'router_w': s(ks[5], (NE, C)), 'w1': s(ks[6], (NE, HID, C)), 'w2': s(ks[7], (NE, C, HID)), 'w3': s(ks[8], (NE, HID, C))}
    _L1_ffn_all = _L1_ffn_setup()
    _L1_ffn_in = {k: v for k, v in _L1_ffn_all.items() if k in ('ln1_w', 'ln2_w', 'wq', 'wk', 'wv', 'wo', 'router_w', 'w1', 'w2', 'w3')}
    del _L1_ffn_all
    return {'x': x, 'cls_tok': cls_tok, 'L0_tok_W': _L0_tok_in['W'], 'L0_tok_b': _L0_tok_in['b'], 'L0_attn_base_phases': _L0_attn_in['base_phases'], 'L0_attn_Wk1': _L0_attn_in['Wk1'], 'L0_attn_bk1': _L0_attn_in['bk1'], 'L0_attn_Wk2': _L0_attn_in['Wk2'], 'L0_attn_bk2': _L0_attn_in['bk2'], 'L0_attn_Wq1': _L0_attn_in['Wq1'], 'L0_attn_bq1': _L0_attn_in['bq1'], 'L0_attn_Wq2': _L0_attn_in['Wq2'], 'L0_attn_bq2': _L0_attn_in['bq2'], 'L0_attn_Wvc': _L0_attn_in['Wvc'], 'L0_attn_bvc': _L0_attn_in['bvc'], 'L0_attn_Wvp': _L0_attn_in['Wvp'], 'L0_attn_bvp': _L0_attn_in['bvp'], 'L0_attn_Wg1': _L0_attn_in['Wg1'], 'L0_attn_bg1': _L0_attn_in['bg1'], 'L0_attn_Wg2': _L0_attn_in['Wg2'], 'L0_attn_bg2': _L0_attn_in['bg2'], 'L0_attn_ln_g': _L0_attn_in['ln_g'], 'L0_attn_ln_b': _L0_attn_in['ln_b'], 'L0_attn_Wo': _L0_attn_in['Wo'], 'L0_attn_bo': _L0_attn_in['bo'], 'L0_ffn_Wg': _L0_ffn_in['Wg'], 'L0_ffn_bg': _L0_ffn_in['bg'], 'L0_ffn_W1': _L0_ffn_in['W1'], 'L0_ffn_b1': _L0_ffn_in['b1'], 'L0_ffn_W2': _L0_ffn_in['W2'], 'L0_ffn_b2': _L0_ffn_in['b2'], 'L1_attn_nu_log': _L1_attn_in['nu_log'], 'L1_attn_theta_log': _L1_attn_in['theta_log'], 'L1_attn_gamma_log': _L1_attn_in['gamma_log'], 'L1_attn_B_re': _L1_attn_in['B_re'], 'L1_attn_B_im': _L1_attn_in['B_im'], 'L1_attn_C_re': _L1_attn_in['C_re'], 'L1_attn_C_im': _L1_attn_in['C_im'], 'L1_ffn_ln1_w': _L1_ffn_in['ln1_w'], 'L1_ffn_ln2_w': _L1_ffn_in['ln2_w'], 'L1_ffn_wq': _L1_ffn_in['wq'], 'L1_ffn_wk': _L1_ffn_in['wk'], 'L1_ffn_wv': _L1_ffn_in['wv'], 'L1_ffn_wo': _L1_ffn_in['wo'], 'L1_ffn_router_w': _L1_ffn_in['router_w'], 'L1_ffn_w1': _L1_ffn_in['w1'], 'L1_ffn_w2': _L1_ffn_in['w2'], 'L1_ffn_w3': _L1_ffn_in['w3']}

def reference(x, cls_tok, L0_tok_W, L0_tok_b, L0_attn_base_phases, L0_attn_Wk1, L0_attn_bk1, L0_attn_Wk2, L0_attn_bk2, L0_attn_Wq1, L0_attn_bq1, L0_attn_Wq2, L0_attn_bq2, L0_attn_Wvc, L0_attn_bvc, L0_attn_Wvp, L0_attn_bvp, L0_attn_Wg1, L0_attn_bg1, L0_attn_Wg2, L0_attn_bg2, L0_attn_ln_g, L0_attn_ln_b, L0_attn_Wo, L0_attn_bo, L0_ffn_Wg, L0_ffn_bg, L0_ffn_W1, L0_ffn_b1, L0_ffn_W2, L0_ffn_b2, L1_attn_nu_log, L1_attn_theta_log, L1_attn_gamma_log, L1_attn_B_re, L1_attn_B_im, L1_attn_C_re, L1_attn_C_im, L1_ffn_ln1_w, L1_ffn_ln2_w, L1_ffn_wq, L1_ffn_wk, L1_ffn_wv, L1_ffn_wo, L1_ffn_router_w, L1_ffn_w1, L1_ffn_w2, L1_ffn_w3):
    import jax
    import jax.numpy as jnp

    def _L0_tok_ref(x, W, b):
        import jax, jax.numpy as jnp
        import numpy as np
        INV_SQRT2 = 0.7071067811865476

        def haar_dwt2(x):
            lo = (x[..., ::2] + x[..., 1::2]) * INV_SQRT2
            hi = (x[..., ::2] - x[..., 1::2]) * INV_SQRT2
            cA = (lo[..., ::2, :] + lo[..., 1::2, :]) * INV_SQRT2
            cH = (lo[..., ::2, :] - lo[..., 1::2, :]) * INV_SQRT2
            cV = (hi[..., ::2, :] + hi[..., 1::2, :]) * INV_SQRT2
            cD = (hi[..., ::2, :] - hi[..., 1::2, :]) * INV_SQRT2
            return (cA, (cH, cV, cD))

        def wavedec2_maps(x, levels):
            a = x
            details = []
            for _ in range(levels):
                a, d = haar_dwt2(a)
                details.append(d)
            maps = [a]
            for d in reversed(details):
                maps.extend(d)
            return maps
        imgs = x[:, 0]
        B = imgs.shape[0]
        maps = wavedec2_maps(imgs, 2)
        proc = [jax.image.resize(m, (B, 8, 8), method='bilinear') for m in maps]
        feat = jnp.stack(proc, axis=1)
        feat = feat.reshape(B, feat.shape[1], 64).transpose(0, 2, 1)
        return feat @ W + b

    def _L0_attn_ref(x, base_phases, Wk1, bk1, Wk2, bk2, Wq1, bq1, Wq2, bq2, Wvc, bvc, Wvp, bvp, Wg1, bg1, Wg2, bg2, ln_g, ln_b, Wo, bo):
        import jax, jax.numpy as jnp
        import numpy as np
        import math
        D = 64
        K = 32
        B = 2
        L = 512
        MAX_SEQ = 2048
        PI = math.pi

        def _content_stream(x, Wk1, bk1, Wk2, bk2, Wq1, bq1, Wq2, bq2, Wvc, bvc):
            Bc, Lc, Dc = x.shape
            key_phase = jnp.tanh(jnp.tanh(x @ Wk1 + bk1) @ Wk2 + bk2) * PI
            query_phase = jnp.tanh(jnp.tanh(x @ Wq1 + bq1) @ Wq2 + bq2) * PI
            value = x @ Wvc + bvc
            cos_k = jnp.cos(key_phase)[..., None]
            sin_k = jnp.sin(key_phase)[..., None]
            v_e = value[:, :, None, :]
            mem_real = jnp.cumsum(cos_k * v_e, axis=1)
            mem_imag = jnp.cumsum(sin_k * v_e, axis=1)
            cos_q = jnp.cos(query_phase)[..., None]
            sin_q = jnp.sin(query_phase)[..., None]
            retrieved = (mem_real * cos_q + mem_imag * sin_q).sum(axis=2)
            positions = jnp.arange(1, Lc + 1, dtype=jnp.float32)
            norm = jnp.sqrt(positions * K)[None, :, None]
            return retrieved / norm

        def _pos_stream(x, base_phases, Wvp, bvp):
            Bc, Lc, Dc = x.shape
            phases = base_phases[:Lc][None]
            value = x @ Wvp + bvp
            cos_p = jnp.cos(phases)
            sin_p = jnp.sin(phases)
            mem_real = jnp.cumsum(value * cos_p, axis=1)
            mem_imag = jnp.cumsum(value * sin_p, axis=1)
            retrieved = mem_real * cos_p + mem_imag * sin_p
            positions = jnp.arange(1, Lc + 1, dtype=jnp.float32)
            return retrieved / jnp.sqrt(positions)[None, :, None]
        pos_retrieved = _pos_stream(x, base_phases, Wvp, bvp)
        content_retrieved = _content_stream(x, Wk1, bk1, Wk2, bk2, Wq1, bq1, Wq2, bq2, Wvc, bvc)
        gates = jax.nn.softmax(jax.nn.relu(x @ Wg1 + bg1) @ Wg2 + bg2, axis=-1)
        combined = gates[:, :, 0:1] * pos_retrieved + gates[:, :, 1:2] * content_retrieved
        mu = combined.mean(axis=-1, keepdims=True)
        var = ((combined - mu) ** 2).mean(axis=-1, keepdims=True)
        normed = (combined - mu) / jnp.sqrt(var + 1e-05) * ln_g + ln_b
        return x + normed @ Wo + bo

    def _L0_ffn_ref(x, Wg, bg, W1, b1, W2, b2):
        import jax, jax.numpy as jnp
        import numpy as np
        B, S, D, H, E, K = (8, 2048, 64, 256, 8, 2)
        gate_scores = jnp.einsum('bsd,ed->bse', x, Wg) + bg
        topk_scores, topk_idx = jax.lax.top_k(gate_scores, K)
        topk_probs = jax.nn.softmax(topk_scores, axis=-1)
        combine = jnp.sum(topk_probs[..., None] * jax.nn.one_hot(topk_idx, E, dtype=x.dtype), axis=-2)
        out = jnp.zeros_like(x)
        for e in range(E):
            h = jax.nn.relu(jnp.einsum('bsd,hd->bsh', x, W1[e]) + b1[e])
            y = jnp.einsum('bsh,dh->bsd', h, W2[e]) + b2[e]
            out = out + combine[..., e:e + 1] * y
        return out

    def _L1_attn_ref(x, nu_log, theta_log, gamma_log, B_re, B_im, C_re, C_im):
        import jax, jax.numpy as jnp
        import numpy as np
        import math
        STATE_DIM = 64
        R_MIN, R_MAX = (0.4, 0.9)
        PHASE_MAX = 2.0 * math.pi
        BATCH, SEQ = (8, 1024)

        def _binop(e_i, e_j):
            a_i, b_i = e_i
            a_j, b_j = e_j
            return (a_j * a_i, a_j * b_i + b_j)
        L_mod = jnp.exp(-jnp.exp(nu_log))
        theta = jnp.exp(theta_log)
        L_diag = (L_mod * jnp.cos(theta) + 1j * L_mod * jnp.sin(theta)).astype(jnp.complex64)
        B = (B_re + 1j * B_im).astype(jnpp.complex64) if False else (B_re + 1j * B_im).astype(jnp.complex64)
        C = (C_re + 1j * C_im).astype(jnp.complex64)
        B_norm = B * jnp.exp(gamma_log)[:, None]
        B_elems = x.astype(jnp.complex64) @ B_norm.T
        L_elems = jnp.broadcast_to(L_diag, B_elems.shape)
        _, inner_states = jax.lax.associative_scan(_binop, (L_elems, B_elems), axis=1)
        return (inner_states @ C.T).real

    def _L1_ffn_ref(x, ln1_w, ln2_w, wq, wk, wv, wo, router_w, w1, w2, w3):
        import jax, jax.numpy as jnp
        import numpy as np
        B, T, C = (64, 96, 64)
        NH, NKV = (4, 2)
        HD = C // NH
        NREP = NH // NKV
        NE, TOPK = (8, 2)
        HID = int(8 / 3 * C)
        EPS_RMS = 1e-06

        def _rope_tables(t_len):
            inv_freq = 1.0 / 10000.0 ** (np.arange(0, HD, 2, dtype=np.float32) / HD)
            t = np.arange(t_len, dtype=np.float32)
            freqs = np.outer(t, inv_freq)
            emb = np.concatenate([freqs, freqs], axis=-1)
            return (jnp.asarray(np.cos(emb)), jnp.asarray(np.sin(emb)))

        def _rotate_half(x):
            h = x.shape[-1] // 2
            return jnp.concatenate([-x[..., h:], x[..., :h]], axis=-1)

        def _rmsnorm(v, w):
            return v * jax.lax.rsqrt(jnp.mean(v * v, axis=-1, keepdims=True) + EPS_RMS) * w
        Bx, Tx, Cx = x.shape
        h = _rmsnorm(x, ln1_w)
        q = (h @ wq.T).reshape(Bx, Tx, NH, HD).transpose(0, 2, 1, 3)
        k = (h @ wk.T).reshape(Bx, Tx, NKV, HD).transpose(0, 2, 1, 3)
        v = (h @ wv.T).reshape(Bx, Tx, NKV, HD).transpose(0, 2, 1, 3)
        cos, sin = _rope_tables(Tx)
        cos, sin = (cos[None, None], sin[None, None])
        q = q * cos + _rotate_half(q) * sin
        k = k * cos + _rotate_half(k) * sin
        k = jnp.repeat(k, NREP, axis=1)
        v = jnp.repeat(v, NREP, axis=1)
        scores = jnp.einsum('bhtd,bhsd->bhts', q, k) / jnp.sqrt(jnp.float32(HD))
        causal = jnp.tril(jnp.ones((Tx, Tx), dtype=bool))
        scores = jnp.where(causal[None, None], scores, jnp.float32(-1e+30))
        att = jax.nn.softmax(scores, axis=-1)
        y = jnp.einsum('bhts,bhsd->bhtd', att, v).transpose(0, 2, 1, 3).reshape(Bx, Tx, Cx)
        x = x + y @ wo.T
        flat = _rmsnorm(x, ln2_w).reshape(-1, Cx)
        probs = jax.nn.softmax(flat @ router_w.T, axis=-1)
        tp, ti = jax.lax.top_k(probs, TOPK)
        tp = tp / (jnp.sum(tp, axis=-1, keepdims=True) + 1e-09)
        weights = jnp.sum(tp[..., None] * jax.nn.one_hot(ti, NE, dtype=flat.dtype), axis=1)
        out = jnp.zeros_like(flat)
        for e in range(NE):
            hh = jax.nn.silu(flat @ w1[e].T) * (flat @ w3[e].T)
            out = out + weights[:, e:e + 1] * (hh @ w2[e].T)
        return x + out.reshape(Bx, Tx, Cx)
    h = _L0_tok_ref(x, L0_tok_W, L0_tok_b)
    h = jnp.concatenate([jnp.broadcast_to(cls_tok, (h.shape[0], 1, h.shape[2])), h], axis=1)
    h = h + _L0_attn_ref(_layernorm(h, axis=-1), L0_attn_base_phases, L0_attn_Wk1, L0_attn_bk1, L0_attn_Wk2, L0_attn_bk2, L0_attn_Wq1, L0_attn_bq1, L0_attn_Wq2, L0_attn_bq2, L0_attn_Wvc, L0_attn_bvc, L0_attn_Wvp, L0_attn_bvp, L0_attn_Wg1, L0_attn_bg1, L0_attn_Wg2, L0_attn_bg2, L0_attn_ln_g, L0_attn_ln_b, L0_attn_Wo, L0_attn_bo)
    h = h + _L0_ffn_ref(_layernorm(h, axis=-1), L0_ffn_Wg, L0_ffn_bg, L0_ffn_W1, L0_ffn_b1, L0_ffn_W2, L0_ffn_b2)
    h = h + _L1_attn_ref(_layernorm(h, axis=-1), L1_attn_nu_log, L1_attn_theta_log, L1_attn_gamma_log, L1_attn_B_re, L1_attn_B_im, L1_attn_C_re, L1_attn_C_im)
    h = h + _L1_ffn_ref(_layernorm(h, axis=-1), L1_ffn_ln1_w, L1_ffn_ln2_w, L1_ffn_wq, L1_ffn_wk, L1_ffn_wv, L1_ffn_wo, L1_ffn_router_w, L1_ffn_w1, L1_ffn_w2, L1_ffn_w3)
    return h

_drawn_inputs = setup_inputs


def setup_inputs(seed=0):
    import zlib

    import numpy as np

    out = dict(_drawn_inputs(seed))
    spreads = {'L0_tok_b': (0.0, 0.1),
     'L0_attn_bk1': (0.0, 0.8),
     'L0_attn_bk2': (0.0, 0.8),
     'L0_attn_bq1': (0.0, 0.8),
     'L0_attn_bq2': (0.0, 0.8),
     'L0_attn_bvc': (0.0, 0.1),
     'L0_attn_bvp': (0.0, 0.8),
     'L0_attn_bg1': (0.0, 0.8),
     'L0_attn_bg2': (0.0, 0.8),
     'L0_attn_ln_g': (1.0, 0.2),
     'L0_attn_ln_b': (0.0, 0.501),
     'L0_attn_bo': (0.0, 0.1),
     'L1_ffn_ln1_w': (1.0, 0.6),
     'L1_ffn_ln2_w': (1.0, 0.6)}
    factors = {'L0_attn_base_phases': 8.0,
     'L0_attn_Wk1': 8.0,
     'L0_attn_Wk2': 8.0,
     'L0_attn_Wq1': 8.0,
     'L0_attn_Wq2': 8.0,
     'L0_attn_Wvp': 7.784,
     'L0_attn_Wg1': 8.0,
     'L0_attn_Wg2': 8.0,
     'L0_ffn_bg': 2.912,
     'L0_ffn_b1': 3.106,
     'L1_ffn_wq': 8.0,
     'L1_ffn_wk': 8.0,
     'L1_ffn_wv': 8.0,
     'L1_ffn_wo': 8.0,
     'L1_ffn_router_w': 8.0,
     'L1_ffn_w1': 8.0,
     'L1_ffn_w2': 8.0,
     'L1_ffn_w3': 8.0}
    for name, (base, spread) in spreads.items():
        noise = np.random.default_rng([zlib.crc32(name.encode()), seed]).standard_normal(out[name].shape)
        drawn = base * np.exp(spread * noise) if base else spread * noise
        out[name] = jnp.asarray(drawn.astype(out[name].dtype))
    for name, factor in factors.items():
        out[name] = (out[name] * factor).astype(out[name].dtype)
    return out
```

```python
import numpy as np
import concourse.bass as bass
from concourse import mybir
from contextlib import ExitStack

F32 = mybir.dt.float32
F32R = mybir.dt.float32r
ALU = mybir.AluOpType
ACT = mybir.ActivationFunctionType
AX = mybir.AxisListType

B = 128
D = 64
L = 65
T = 5
NT = L // T
TOK = T * B
HALF = TOK // 2
E = 8
BG = 8
NBG = B // BG
IMG = 96
GRID = 8
PI = float(np.pi)
PI_BELOW = float(np.nextafter(np.float32(np.pi), np.float32(0)) if np.float32(np.pi) > np.pi else np.float32(np.pi))
EPS_LN = 1e-5
EPS_RMS = 1e-6


def need(eng, sem, value):
    if not isinstance(value, int) or value > 0:
        eng.wait_ge(sem, value)


def take_waits(eng, taken):
    eng.sem_inc(taken, 1)


class Room:

    def __init__(self, nc, ctx, phase):
        self.nc, self.ctx, self.phase, self.mine = nc, ctx, phase, []
        ctx.callback(self.hand_back)

    def sb(self, name, shape, dt=F32):
        return self.ctx.enter_context(self.nc.sbuf_tensor(f"{self.phase}_{name}", shape, dt))

    def ps(self, name, rows, cols):
        banks = -(-cols // 512)
        return self.ctx.enter_context(self.nc.psum_tensor(f"{self.phase}_{name}", [rows, banks * 512], F32))

    def sems(self, names):
        new = [self.nc.alloc_semaphore(f"{self.phase}_{n}") for n in names.split()]
        self.mine += new
        return new

    def hand_back(self):
        self.nc.clear_and_free_semaphores(self.mine)
        self.nc.all_engine_barrier()


class Chain:

    def __init__(self, eng, sem):
        self.eng, self.sem, self.total, self.k, self.i, self.per = eng, sem, 0, 0, 0, 0

    def enter(self, i, per):
        self.i, self.per, self.k = i, per, 0

    def leave(self, steps):
        assert self.k == self.per, (self.k, self.per)
        self.total, self.i, self.k, self.per = self.total + steps * self.per, 0, 0, 0

    def leave_straight(self):
        assert not self.per
        self.total, self.k = self.total + self.k, 0

    def link(self, ins):
        ins.then_inc(self.sem, 1)
        self.k += 1
        self.eng.wait_ge(self.sem, self.i * self.per + (self.total + self.k))


    def spread(self, ins):
        ins.then_inc(self.sem, 1)
        self.k += 1
        mine = self.i * self.per + (self.total + self.k)
        yield
        self.eng.wait_ge(self.sem, mine)


def norm_statistics(dve, chain, src, cen, sq, stats, rstd_asked, eps=EPS_LN):
    mean, var = stats[:, 0, :], stats[:, 1, :]
    chain.link(dve.tensor_reduce(mean, src, axis=AX.X, op=ALU.add))
    chain.link(dve.tensor_scalar(mean, mean, 1.0 / D, None, ALU.mult))
    chain.link(dve.tensor_tensor(cen, src, over_width(mean), ALU.subtract))
    chain.link(dve.tensor_tensor(sq, cen, cen, ALU.mult))
    chain.link(dve.tensor_reduce(var, sq, axis=AX.X, op=ALU.add))
    dve.tensor_scalar(var, var, 1.0 / D, eps, ALU.mult, ALU.add).then_inc(rstd_asked, 1)


NORM_LINKS = 5


def over_width(per_token):
    return per_token.unsqueeze(2).to_broadcast([B, T, D])


def rstd_step(pool, stats, minus_half, rstd_asked, rstd_ready, n):
    pool.wait_ge(rstd_asked, n)
    pool.tensor_tensor(stats[:, 2, :], stats[:, 1, :], minus_half[:, 0:T], ALU.pow).then_inc(rstd_ready, 1)



SPLIT = 128
HID0 = 256
HID1 = 170
REST1 = HID1 - SPLIT
CH0 = HID0 // SPLIT * E
CH1 = 3 * E // 2
NH, HD = 4, 16

EARLY = dict(rowsT=32, tokW=512, tokb=512, cls=D, wkq1=128, wkq2=128, bkq2=1, wg1=16, wg2=2, wvc=D,
             wvp=128, phase=L, wo0=D, lng=1, lnb=1, ident=B, stack2=D, quarter=1, half_pi=1,
             feat_sign=1, sin_scale=1, sin_bias=1, causal0=L, pos_norm=L, descend=T * E)
LATE = dict(up0=CH0 * SPLIT, down0=2 * E * D, gate0=E, gbias0=E, b1=CH0, b2=E // 2,
            up1=2 * CH1 * SPLIT, down1=2 * E * D, gate1=E, ln1=1, ln2=D,
            bT=128, gamma=128, nu=1, theta=1, cT=D, c_sign=1, rotJ=128,
            wqx=128, wkx=128, fold=128, ropeq=L, ropek=L, wv=32, wo1=D, mask1=L)


def columns(widths):
    out, at = {}, 0
    for name, w in widths.items():
        out[name] = slice(at, at + w)
        at += w
    return out, at


def tokenizer(nc, x, dram_early, dram_late, early, late, h, minus_half):
    NR = 32
    CI = 8
    NBUF = 4
    ROUNDS = B // (NBUF * 2 * CI)
    ec, _ = columns(EARLY)
    with ExitStack() as ctx:
        def sb(name, shape, dt=F32):
            return ctx.enter_context(nc.sbuf_tensor(name, shape, dt))

        def sem(name):
            return ctx.enter_context(nc.semaphore(name))
        images = [sb(f"images{k}", [IMG, 2 * CI, IMG]) for k in range(NBUF)]
        Y = sb("rows_done", [IMG, NR, B])
        Z = sb("maps", [128, GRID * B])
        psY = [ctx.enter_context(nc.psum_tensor(f"ps_rows{k}", [IMG, CI, NR], F32)) for k in range(2)]
        psZ = ctx.enter_context(nc.psum_tensor("ps_cols", [128, GRID * B], F32))
        psH = [ctx.enter_context(nc.psum_tensor(f"ps_tok{k}", [128, GRID * D], F32)) for k in range(2)]
        rows_in, early_in, late_in = sem("rows_in"), sem("early_in"), sem("late_in")
        x_in = [sem(f"x_in{k}") for k in range(NBUF)]
        rows_mm = [sem(f"rows_mm{k}") for k in range(2)]
        rows_out = [sem(f"rows_out{k}") for k in range(2)]
        cols_mm, cols_out, tok_mm, tok_out, cls_out, half_set = (
            sem(n) for n in ("cols_mm", "cols_out", "tok_mm", "tok_out", "cls_out", "half_set"))
        with nc.Block() as block:
            @block.sync
            def _(sp):
                sp.dma_start(early[:, ec["rowsT"]], dram_early[:, ec["rowsT"]]).then_inc(rows_in, 16)
                def load(n, k):
                    for rows in rows_mm:
                        need(sp, rows, (n - 1) * NBUF + k + 1)
                    at = (n * NBUF + k) * 2 * CI
                    sp.dma_start(images[k][:, :, :], x[:, at:at + 2 * CI, :]).then_inc(x_in[k], 16)

                for k in range(NBUF):
                    load(0, k)
                rest = slice(ec["rowsT"].stop, None)
                sp.dma_start(early[:, rest], dram_early[:, rest]).then_inc(early_in, 16)
                for n in range(1, ROUNDS):
                    for k in range(NBUF):
                        load(n, k)
                sp.wait_ge(late_in, 16)

            @block.gpsimd
            def _(pool):
                pool.memset(minus_half[:, :], -0.5).then_inc(half_set, 1)
                pool.wait_ge(x_in[NBUF - 1], 16)
                pool.dma_start(late[:, :], dram_late).then_inc(late_in, 16)

            @block.tensor
            def _(pe):
                pe.wait_ge(rows_in, 16)
                with pe.Fori(0, ROUNDS) as n:
                    for k in range(NBUF):
                        pe.wait_ge(x_in[k], (n + 1) * 16)
                        for p in range(2):
                            pe.wait_ge(rows_out[p], n * NBUF + k)
                            for b in range(CI):
                                last = pe.matmul(psY[p][:, b, :], images[k][:, p * CI + b, :], early[0:IMG, ec["rowsT"]],
                                                 start=True, stop=True)
                            last.then_inc(rows_mm[p], 1)
                for p in range(2):
                    pe.wait_ge(rows_out[p], ROUNDS * NBUF)
                for rt in range(4):
                    src = Y[:, rt * GRID:(rt + 1) * GRID, :].rearrange("c i b -> c (i b)")
                    for half in range(2):
                        last = pe.matmul(psZ[rt * 32:(rt + 1) * 32, half * 512:(half + 1) * 512],
                                         early[0:IMG, ec["rowsT"]], src[:, half * 512:(half + 1) * 512],
                                         start=True, stop=True)
                last.then_inc(cols_mm, 1)
                pe.wait_ge(cols_out, 2)
                pe.wait_ge(early_in, 16)
                for i in range(GRID):
                    need(pe, tok_out, i - 1)
                    pe.matmul(psH[i % 2][:, :], Z[:, i * B:(i + 1) * B], early[:, ec["tokW"]],
                              start=True, stop=True).then_inc(tok_mm, 1)

            @block.scalar
            def _(act):
                act.wait_ge(cols_mm, 1)
                act.copy(Z[:, 0:512], psZ[:, 0:512]).then_inc(cols_out, 1)

            @block.vector
            def _(dve):
                with dve.Fori(0, ROUNDS * NBUF) as n:
                    for p in range(2):
                        dve.wait_ge(rows_mm[p], n + 1)
                        dve.tensor_copy(Y[:, :, bass.ds((n * 2 + p) * CI, CI)],
                                        psY[p][:, :, :].rearrange("c b r -> c r b")).then_inc(rows_out[p], 1)
                dve.wait_ge(cols_mm, 1)
                dve.tensor_copy(Z[:, 512:1024], psZ[:, 512:1024]).then_inc(cols_out, 1)
                dve.wait_ge(early_in, 16)
                dve.tensor_copy(h[:, 0, :], early[:, ec["cls"]]).then_inc(cls_out, 1)
                for i in range(GRID):
                    dve.wait_ge(tok_mm, i + 1)
                    dve.tensor_tensor(h[:, 1 + GRID * i:1 + GRID * (i + 1), :].rearrange("p j d -> p (j d)"),
                                      psH[i % 2][:, :], early[:, ec["tokb"]], ALU.add).then_inc(tok_out, 1)


def tiles(t, g):
    return t[:, bass.ds(g * TOK, TOK)]


def pieces():
    return [(0, 512), (512, TOK - 512)]


def attention0(nc, early, h, n_all, minus_half):
    c, _ = columns(EARLY)
    with ExitStack() as ctx:
        sb = Room(nc, ctx, "attention0").sb
        nT = sb("nT", [D + 1, L * B])
        phi = sb("phi", [128, L * B])
        gate_diff = sb("gate_diff", [B, L])
        gates = sb("gates", [B, 2, L])
        cs = sb("cs", [128, L])
        cs_diag = sb("cs_diag", [128, L, D])
        project0(nc, early, c, h, n_all, minus_half, nT, phi, gate_diff)
        content0(nc, early, c, nT, phi, gate_diff, gates, cs, cs_diag)
        combine0(nc, early, c, h, n_all, minus_half, nT, phi, gates, cs, cs_diag)


def project0(nc, early, c, h, n_all, minus_half, nT, phi, gate_diff):
    with ExitStack() as ctx:
        room = Room(nc, ctx, "project0")
        sb, ps = room.sb, room.ps
        n_tile = sb("n_tile", [B, T, D])
        cen, sq, stats = sb("cen", [B, T, D]), sb("sq", [B, T, D]), sb("stats", [B, 3, T])
        tanh1 = sb("tanh1", [128, TOK])
        tanh2 = sb("tanh2", [128, TOK])
        gate_h = sb("gate_h", [32, TOK])
        logits = sb("logits", [B, T, 2])
        first = sb("first", [1, 2])
        shared = ps("psTL", B, 1024)
        psT, psL = shared[0:64, 0:TOK], shared[:, TOK:TOK + 2 * T]
        psG, psA, psB = ps("psG", 16, TOK), ps("psA", 128, TOK), ps("psB", 128, TOK)
        (p_step, p_rstd_asked, p_rstd, p_n, p_kept, p_T, p_nT, p_A, p_tanh1, p_B, p_tanh2, p_abs, p_G, p_relu,
         p_L, p_diff, p_ones, p_taken, p_first, p_table) = room.sems("step rstd_asked rstd n kept T nT A tanh1 B tanh2 abs G relu L diff ones taken first table")
        act_taken, = room.sems("act_taken")
        with nc.Block() as block:
            @block.gpsimd
            def _(pool):
                pool.memset(nT[D:D + 1, :], 1.0).then_inc(p_ones, 1)
                pool.memset(gate_h[:, :], 1.0).then_inc(p_ones, 1)
                pool.memset(first[:, 0:1], 0.0).then_inc(p_first, 1)
                with pool.Fori(0, NT) as g:
                    rstd_step(pool, stats, minus_half, p_rstd_asked, p_rstd, g + 1)

            @block.vector
            def _(dve):
                chain = Chain(dve, p_step)

                def norm(g):
                    norm_statistics(dve, chain, h[:, bass.ds(g * T, T), :], cen[:, :, :], sq[:, :, :], stats, p_rstd_asked)
                    dve.wait_ge(p_rstd, g + 1)
                    need(dve, p_T, g)
                    need(dve, p_kept, g)
                    dve.tensor_tensor(n_tile[:, :, :], cen[:, :, :], over_width(stats[:, 2, :]), ALU.mult).then_inc(p_n, 1)

                def relu(g):
                    dve.wait_ge(p_G, g + 1)
                    need(dve, p_L, g)
                    dve.tensor_scalar(gate_h[0:16, :], psG[:, 0:TOK], 0.0, None, ALU.max).then_inc(p_relu, 1)

                def phase(g):
                    dve.wait_ge(p_tanh2, g + 1)
                    dve.scalar_tensor_tensor(tiles(phi, g), tanh2[:, :], early[:, c["feat_sign"]], tanh2[:, :],
                                             ALU.mult, ALU.max).then_inc(p_abs, 1)
                    dve.wait_ge(p_L, g + 1)
                    need(dve, p_diff, g)
                    chain.link(dve.tensor_copy(logits[:, :, :], psL[:, 0:2 * T].rearrange("b (t k) -> b t k", k=2)))
                    dve.tensor_tensor(gate_diff[:, bass.ds(g * T, T)], logits[:, :, 0], logits[:, :, 1],
                                      ALU.subtract).then_inc(p_diff, 1)

                def step(g, ahead):
                    relu(g)
                    if ahead:
                        norm(g + 2)
                    phase(g)

                dve.wait_ge(p_ones, 2)
                for g in range(2):
                    chain.enter(0, NORM_LINKS)
                    norm(g)
                    chain.leave(1)
                with dve.Fori(0, NT - 2) as g:
                    chain.enter(g, NORM_LINKS + 1)
                    step(g, True)
                chain.leave(NT - 2)
                for g in range(NT - 2, NT):
                    chain.enter(0, 1)
                    step(g, False)
                    chain.leave(1)

            @block.scalar
            def _(act):
                def keep_norm(g):
                    act.wait_ge(p_n, g + 1)
                    take_waits(act, act_taken)
                    act.copy(n_all[:, bass.ds(g * T, T), :], n_tile[:, :, :]).then_inc(p_kept, 1)
                    act.wait_ge(p_T, g + 1)
                    take_waits(act, act_taken)
                    act.copy(nT[0:D, bass.ds(g * TOK, TOK)], psT[:, 0:TOK]).then_inc(p_nT, 1)

                def step(g, more):
                    act.wait_ge(p_A, g + 1)
                    need(act, p_B, g)
                    act.activation(tanh1[:, :], psA[:, 0:TOK], ACT.Tanh).then_inc(p_tanh1, 1)
                    if more:
                        keep_norm(g + 1)
                    act.wait_ge(p_B, g + 1)
                    need(act, p_abs, g)
                    act.activation(tanh2[:, :], psB[:, 0:TOK], ACT.Tanh, bias=early[:, c["bkq2"]]).then_inc(p_tanh2, 1)

                act.wait_ge(p_first, 1)
                act.activation(first[:, 1:2], first[:, 0:1], ACT.Tanh).then_inc(p_table, 1)
                keep_norm(0)
                with act.Fori(0, NT - 1) as g:
                    step(g, True)
                step(NT - 1, False)

            @block.tensor
            def _(pe):
                def transposes(g):
                    pe.wait_ge(p_n, g + 1)
                    need(pe, p_nT, g)
                    need(pe, p_diff, g - 1)
                    take_waits(pe, p_taken)
                    for t in range(T):
                        last = pe.transpose(psT[:, t * B:(t + 1) * B], n_tile[:, t, :], early[:, c["ident"]])
                    last.then_inc(p_T, 1)

                def first_layer(g):
                    pe.wait_ge(p_nT, g + 1)
                    need(pe, p_tanh1, g)
                    for at, n in pieces():
                        last = pe.matmul(psA[:, at:at + n], early[0:D + 1, c["wkq1"]],
                                         nT[:, bass.ds(g * TOK + at, n)], start=True, stop=True)
                    last.then_inc(p_A, 1)

                def gates_first_layer(g):
                    pe.wait_ge(p_nT, g + 1)
                    need(pe, p_relu, g)
                    take_waits(pe, p_taken)
                    for at, n in pieces():
                        last = pe.matmul(psG[:, at:at + n], early[0:D + 1, c["wg1"]],
                                         nT[:, bass.ds(g * TOK + at, n)], start=True, stop=True)
                    last.then_inc(p_G, 1)

                def second_layer(g):
                    pe.wait_ge(p_tanh1, g + 1)
                    need(pe, p_tanh2, g)
                    for at, n in pieces():
                        last = pe.matmul(psB[:, at:at + n], early[:, c["wkq2"]], tanh1[:, at:at + n],
                                         start=True, stop=True)
                    last.then_inc(p_B, 1)

                def gates_second_layer(g, more):
                    pe.wait_ge(p_relu, g + 1)
                    need(pe, p_diff, g)
                    if more:
                        pe.wait_ge(p_nT, g + 2)
                    for t in range(T):
                        last = pe.matmul(psL[:, 2 * t:2 * t + 2], gate_h[0:17, t * B:(t + 1) * B],
                                         early[0:17, c["wg2"]], start=True, stop=True)
                    last.then_inc(p_L, 1)

                def step(g, more):
                    gates_first_layer(g)
                    if more:
                        transposes(g + 1)
                    second_layer(g)
                    gates_second_layer(g, more)
                    if more:
                        first_layer(g + 1)

                pe.wait_ge(p_ones, 2)
                transposes(0)
                first_layer(0)
                with pe.Fori(0, NT - 1) as g:
                    step(g, True)
                step(NT - 1, False)


def reduced_angle(dve, chain, ang, turns, quarter, half_pi):
    two_pi = (6.28125, 1.93500518798828125e-3, float(2 * np.pi - 6.28125 - 1.93500518798828125e-3))
    magic = 1.5 * 2 ** 23
    chain.link(dve.tensor_scalar(turns, ang, 1 / (2 * PI), quarter, ALU.mult, ALU.add))
    chain.link(dve.tensor_scalar(turns, turns, magic, None, ALU.add))
    chain.link(dve.tensor_scalar(turns, turns, magic, None, ALU.subtract))
    for part in two_pi:
        chain.link(dve.scalar_tensor_tensor(ang, turns, -part, ang, ALU.mult, ALU.add))
    chain.link(dve.tensor_scalar(ang, ang, half_pi, PI_BELOW, ALU.add, ALU.min))
    chain.link(dve.tensor_scalar(ang, ang, -PI_BELOW, None, ALU.max))


def content0(nc, early, c, nT, phi, gate_diff, gates, cs, cs_diag):
    HB = BG // 2
    with ExitStack() as ctx:
        room = Room(nc, ctx, "content0")
        sb, ps = room.sb, room.ps
        kf, qf = sb("key_feat", [64, BG, L]), sb("query_feat", [64, BG, L])
        nTb = sb("nT_batches", [D + 1, BG, L])
        val, score = sb("values", [L, BG, D]), sb("scores", [L, BG, L])
        ang, turns = sb("ang", [128, L]), sb("turns", [128, L])
        cs_norm, th = sb("cs_norm", [128, L]), sb("gate_tanh", [B, L])
        psV, psS, psO = ps("psV", L, BG * D), ps("psS", L, 1024), ps("psO", D, 1024)
        psV = psV[:, :].rearrange("s (b d) -> s b d", d=D)
        psS = psS[:, :].rearrange("s (k n) -> s k n", k=2)
        psO = psO[:, :].rearrange("d (k n) -> d k n", k=2)
        (c_step, c_feat, c_nTb, c_V, c_val, c_S, c_score, c_O, c_out, c_ang, c_cs, c_tanh, c_tab) = room.sems(
            "step feat nTb V val S score O out ang cs tanh tab")

        def batches(t, i, rows=slice(0, 64)):
            return t[rows, :].rearrange("p (t b) -> p t b", b=B)[:, :, bass.ds(i * BG, BG)]

        with nc.Block() as block:
            @block.scalar
            def _(act):
                act.activation(th[:, :], gate_diff[:, :], ACT.Tanh, scale=0.5).then_inc(c_tanh, 1)
                act.wait_ge(c_ang, 1)
                act.activation(cs[:, :], ang[:, :], ACT.Sin).then_inc(c_cs, 1)

                def features(i):
                    need(act, c_S, i)
                    for rows, dst in ((slice(0, 64), kf), (slice(64, 128), qf)):
                        act.activation(dst[:, :, :].rearrange("p b t -> p t b"), batches(phi, i, rows), ACT.Sin,
                                       bias=early[rows, c["sin_bias"]], scale=early[rows, c["sin_scale"]]).then_inc(c_feat, 1)

                def values(i):
                    act.wait_ge(c_V, i + 1)
                    need(act, c_O, i)
                    act.copy(val[:, :, :], psV[:, :, :]).then_inc(c_val, 1)

                features(0)
                values(0)
                features(1)
                with act.Fori(0, NBG - 2) as i:
                    values(i + 1)
                    features(i + 2)
                values(NBG - 1)

            @block.tensor
            def _(pe):
                def values(i):
                    pe.wait_ge(c_nTb, i + 1)
                    need(pe, c_val, i)
                    for b in range(BG):
                        last = pe.matmul(psV[:, b, :], nTb[:, b, :], early[0:D + 1, c["wvc"]], start=True, stop=True)
                    last.then_inc(c_V, 1)

                def scores(i):
                    pe.wait_ge(c_feat, i * 2 + 2)
                    need(pe, c_score, i * 2)
                    for b in range(BG):
                        last = pe.matmul(psS[:, b // HB, (b % HB) * L:(b % HB + 1) * L], kf[:, b, :], qf[:, b, :],
                                         start=True, stop=True)
                    last.then_inc(c_S, 1)

                def outputs(i):
                    pe.wait_ge(c_val, i + 1)
                    pe.wait_ge(c_score, i * 2 + 2)
                    need(pe, c_out, i)
                    for b in range(BG):
                        last = pe.matmul(psO[:, b // HB, (b % HB) * L:(b % HB + 1) * L], val[:, b, :], score[:, b, :],
                                         start=True, stop=True)
                    last.then_inc(c_O, 1)

                values(0)
                scores(0)
                with pe.Fori(0, NBG - 1) as i:
                    values(i + 1)
                    outputs(i)
                    scores(i + 1)
                outputs(NBG - 1)

            @block.vector
            def _(dve):
                chain = Chain(dve, c_step)
                chain.link(dve.tensor_copy(ang[:, :], early[:, c["phase"]]))
                reduced_angle(dve, chain, ang[:, :], turns[:, :], early[:, c["quarter"]], early[:, c["half_pi"]])
                dve.sem_inc(c_ang, 1)
                dve.wait_ge(c_tanh, 1)
                dve.tensor_scalar(gates[:, 0, :], th[:, :], 0.5, 0.5, ALU.mult, ALU.add).then_inc(c_tab, 1)
                dve.tensor_scalar(gates[:, 1, :], th[:, :], -0.5, 0.5, ALU.mult, ALU.add).then_inc(c_tab, 1)
                dve.wait_ge(c_cs, 1)
                chain.link(dve.tensor_tensor(cs_norm[:, :], cs[:, :], early[:, c["pos_norm"]], ALU.mult))
                dve.tensor_tensor(cs_diag[:, :, :], early[:, c["stack2"]].unsqueeze(1).to_broadcast([128, L, D]),
                                  cs_norm[:, :].unsqueeze(2).to_broadcast([128, L, D]), ALU.mult).then_inc(c_tab, 1)

                def take_norm(i):
                    need(dve, c_V, i)
                    dve.tensor_copy(nTb[:, :, :].rearrange("p b t -> p t b"), batches(nT, i, slice(0, D + 1))).then_inc(c_nTb, 1)

                def weigh_scores(i):
                    dve.wait_ge(c_S, i + 1)
                    need(dve, c_O, i)
                    for k in range(2):
                        dve.tensor_tensor(score[:, k * HB:(k + 1) * HB, :],
                                          psS[:, k, 0:HB * L].rearrange("s (b t) -> s b t", t=L),
                                          early[0:L, c["causal0"]].unsqueeze(1).to_broadcast([L, HB, L]),
                                          ALU.mult).then_inc(c_score, 1)

                def keep_outputs(i):
                    dve.wait_ge(c_O, i + 1)
                    for k in range(2):
                        out = phi[0:64, :].rearrange("p (t b) -> p b t", b=B)[:, bass.ds(i * BG + k * HB, HB), :]
                        last = dve.tensor_copy(out, psO[:, k, 0:HB * L].rearrange("s (b t) -> s b t", t=L))
                    last.then_inc(c_out, 1)

                take_norm(0)
                take_norm(1)
                with dve.Fori(0, NBG - 2) as i:
                    weigh_scores(i)
                    take_norm(i + 2)
                    keep_outputs(i)
                for i in (NBG - 2, NBG - 1):
                    weigh_scores(i)
                    keep_outputs(i)


def combine0(nc, early, c, h, n_all, minus_half, nT, content, gates, cs, cs_diag):
    with ExitStack() as ctx:
        room = Room(nc, ctx, "combine0")
        sb, ps = room.sb, room.ps
        z = sb("running", [128, T, B])
        ct = sb("content_tile", [64, TOK])
        mix, mix2 = sb("mix", [B, T, D]), sb("mix2", [B, T, D])
        cen, sq, stats = sb("cen", [B, T, D]), sb("sq", [B, T, D]), sb("stats", [B, 3, T])
        normed = sb("normed", [B, T, D])
        normedT = sb("normedT", [D + 1, TOK])
        psP, psN = ps("psP", 128, TOK), ps("psN", 64, TOK)
        psQ, psC, psW = (ps(name, B, T * D)[:, 0:T * D].rearrange("b (t d) -> b t d", d=D)
                         for name in ("psQ", "psC", "psW"))
        (m_step, m_ones, m_P, m_z, m_Q, m_ct, m_C, m_pos, m_con, m_rstd_asked, m_rstd, m_normed, m_N, m_NT,
         m_W, m_sum, m_h, m_taken) = room.sems(
             "step ones P z Q ct C pos con rstd_asked rstd normed N NT W sum h taken")
        act_taken, = room.sems("act_taken")
        with nc.Block() as block:
            @block.gpsimd
            def _(pool):
                pool.memset(normedT[D:D + 1, :], 1.0).then_inc(m_ones, 1)
                with pool.Fori(0, NT) as g:
                    rstd_step(pool, stats, minus_half, m_rstd_asked, m_rstd, g + 1)

            @block.vector
            def _(dve):
                chain = Chain(dve, m_step)

                def sums(g):
                    dve.wait_ge(m_P, g + 1)
                    need(dve, m_Q, g)
                    for t in range(T):
                        ins = dve.scalar_tensor_tensor(z[:, t, :], psP[:, t * B:(t + 1) * B],
                                                       cs[:, bass.ds(g * T + t, 1)], z[:, (t - 1) % T, :],
                                                       ALU.mult, ALU.add)
                        if t < T - 1:
                            chain.link(ins)
                        else:
                            ins.then_inc(m_z, 1)
                    dve.wait_ge(m_z, g + 1)

                def mixing(g, following=None):
                    tile = bass.ds(g * T, T)
                    dve.wait_ge(m_Q, g + 1)
                    dve.tensor_tensor(mix[:, :, :], psQ[:, :, :], over_width(gates[:, 0, tile]), ALU.mult).then_inc(m_pos, 1)
                    dve.wait_ge(m_C, g + 1)
                    dve.tensor_tensor(mix2[:, :, :], psC[:, :, :], over_width(gates[:, 1, tile]), ALU.mult).then_inc(m_con, 1)
                    dve.wait_ge(m_pos, g + 1)
                    dve.wait_ge(m_con, g + 1)
                    chain.link(dve.tensor_tensor(mix[:, :, :], mix[:, :, :], mix2[:, :, :], ALU.add))
                    norm_statistics(dve, chain, mix[:, :, :], cen[:, :, :], sq[:, :, :], stats, m_rstd_asked)
                    if following is not None:
                        sums(following)
                    dve.wait_ge(m_rstd, g + 1)
                    need(dve, m_N, g)
                    dve.tensor_tensor(normed[:, :, :], cen[:, :, :], over_width(stats[:, 2, :]), ALU.mult).then_inc(m_normed, 1)

                def residual(g):
                    tile = bass.ds(g * T, T)
                    dve.wait_ge(m_W, g + 1)
                    need(dve, m_h, g)
                    dve.tensor_tensor(mix2[:, :, :], psW[:, :, :], n_all[:, tile, :], ALU.add).then_inc(m_sum, 1)
                    dve.wait_ge(m_sum, g + 1)
                    dve.tensor_tensor(h[:, tile, :], h[:, tile, :], mix2[:, :, :], ALU.add).then_inc(m_h, 1)
                    dve.wait_ge(m_h, g + 1)

                PER_SUMS, PER_MIX = T - 1, 1 + NORM_LINKS
                chain.enter(0, 1 + PER_SUMS)
                chain.link(dve.memset(z[:, T - 1, :], 0.0))
                sums(0)
                chain.leave(1)
                chain.enter(0, PER_SUMS + PER_MIX)
                mixing(0, 1)
                chain.leave(1)
                with dve.Fori(1, NT - 1) as g:
                    chain.enter(g - 1, PER_SUMS + PER_MIX)
                    mixing(g, g + 1)
                    residual(g - 1)
                chain.leave(NT - 2)
                chain.enter(0, PER_MIX)
                mixing(NT - 1)
                chain.leave(1)
                residual(NT - 2)
                residual(NT - 1)

            @block.scalar
            def _(act):
                def content_tile(g):
                    need(act, m_C, g)
                    take_waits(act, act_taken)
                    act.copy(ct[:, :], content[0:64, bass.ds(g * TOK, TOK)]).then_inc(m_ct, 1)

                def transposed_norm(g):
                    act.wait_ge(m_N, g + 1)
                    need(act, m_W, g)
                    act.activation(normedT[0:D, :], psN[:, 0:TOK], ACT.Identity, bias=early[0:D, c["lnb"]],
                                   scale=early[0:D, c["lng"]]).then_inc(m_NT, 1)

                act.wait_ge(m_ones, 1)
                content_tile(0)
                content_tile(1)
                with act.Fori(0, NT - 2) as g:
                    transposed_norm(g)
                    content_tile(g + 2)
                transposed_norm(NT - 2)
                transposed_norm(NT - 1)

            @block.tensor
            def _(pe):
                ident = early[:, c["ident"]]

                def position_values(g):
                    need(pe, m_z, g)
                    for at, n in pieces():
                        last = pe.matmul(psP[:, at:at + n], early[0:D + 1, c["wvp"]],
                                         nT[:, bass.ds(g * TOK + at, n)], start=True, stop=True)
                    last.then_inc(m_P, 1)

                def streams(g):
                    need(pe, m_pos, g)
                    need(pe, m_con, g)
                    pe.wait_ge(m_ct, g + 1)
                    take_waits(pe, m_taken)
                    for t in range(T):
                        last = pe.transpose(psC[:, t, :], ct[:, t * B:(t + 1) * B], ident[0:64, 0:64])
                    last.then_inc(m_C, 1)
                    pe.wait_ge(m_z, g + 1)
                    for t in range(T):
                        last = pe.matmul(psQ[:, t, :], z[:, t, :], cs_diag[:, bass.ds(g * T + t, 1), :].squeeze(1),
                                         start=True, stop=True)
                    last.then_inc(m_Q, 1)

                def projection(g):
                    pe.wait_ge(m_normed, g + 1)
                    need(pe, m_NT, g)
                    take_waits(pe, m_taken)
                    for t in range(T):
                        last = pe.transpose(psN[:, t * B:(t + 1) * B], normed[:, t, :], ident)
                    last.then_inc(m_N, 1)
                    pe.wait_ge(m_NT, g + 1)
                    need(pe, m_sum, g)
                    for t in range(T):
                        last = pe.matmul(psW[:, t, :], normedT[:, t * B:(t + 1) * B], early[0:D + 1, c["wo0"]],
                                         start=True, stop=True)
                    last.then_inc(m_W, 1)

                pe.wait_ge(m_ones, 1)
                position_values(0)
                streams(0)
                position_values(1)
                with pe.Fori(0, NT - 2) as g:
                    streams(g + 1)
                    position_values(g + 2)
                    projection(g)
                streams(NT - 1)
                projection(NT - 2)
                projection(NT - 1)


OUT_FROM, Y_LATER, LOW_AT = 4, 2, 9
HIDDEN_RING = 8


def top_two(dve, chain, val, room, descend, big):
    eq, ranked, left, best, first, second, m1, m2 = room
    for at, (values, place, top) in enumerate(((val, first, m1), (left, second, m2))):
        over = lambda x: x.unsqueeze(2).to_broadcast([B, T, E])
        yield from chain.spread(dve.tensor_reduce(top, values, axis=AX.X, op=ALU.max))
        yield from chain.spread(dve.tensor_tensor(eq, values, over(top), ALU.is_equal))
        yield from chain.spread(dve.tensor_tensor(ranked, eq, descend, ALU.mult))
        yield from chain.spread(dve.tensor_reduce(best, ranked, axis=AX.X, op=ALU.max))
        yield from chain.spread(dve.tensor_tensor(place, ranked, over(best), ALU.is_equal))
        if at == 0:
            yield from chain.spread(dve.scalar_tensor_tensor(left, place, -big, values, ALU.mult, ALU.add))


TOP_TWO_LINKS = 11


def moe(nc, layer, late, early, src, resid, out, minus_half):
    c, ec = columns(LATE)[0], columns(EARLY)[0]
    up_cols, down_cols, gate_cols = (c[f"{k}{layer}"] for k in ("up", "down", "gate"))
    NUP = up_cols.stop - up_cols.start
    PAIRS = E // 2
    CPP = 4 if layer == 0 else 3
    UPG = PAIRS * 2 * CPP
    with ExitStack() as ctx:
        room = Room(nc, ctx, f"moe{layer}")
        sb, ps = room.sb, room.ps
        w_hi, w_lo = sb("w_hi", [128, NUP + E], F32R), sb("w_lo", [128, NUP + E], F32R)
        nTr = sb("nT_parts", [128, L * B], F32R)
        nT_tile = sb("nT_tile", [128, TOK], F32R)
        nrm, split = sb("nrm", [B, T, D]), sb("split", [B, T, 128])
        cen, sq, stats = sb("cen", [B, T, D]), sb("sq", [B, T, D]), sb("stats", [B, 3, T])
        hid = [sb(f"hid{k}", [128, HALF]) for k in range(HIDDEN_RING)]
        sil = [sb(f"silu{k}", [128, HALF]) for k in range(4)] if layer else None
        y = sb("y", [128, PAIRS, TOK])
        scaled = sb("scaled", [B, T, E * D])
        sum4, sum2, sum1 = sb("sum4", [B, T, 4 * D]), sb("sum2", [B, T, 2 * D]), sb("sum1", [B, T, D])
        weights = sb("weights", [B, L, E])
        small = {k: sb("r_" + k, [B, T, E]) for k in "val eq ranked left first second d prob a".split()}
        tiny = {k: sb("r_" + k, [B, T]) for k in "m0 m1 m2 best diff ex den rec w2 sum".split()}
        if layer == 1:
            base = sb("base", [B, T, E])
            base_set, = room.sems("base_set")
        psU = [ps(f"psU{k}", 128, HALF) for k in range(4)]
        psY = [ps(f"psY{k}", 128, HALF) for k in range(2)]
        psM = ps("psM", 128, TOK)
        (step, w_hi_set, w_lo_set, rstd_asked, rstd, n_set, hi_set, lo_set, T_mm, nTr_set, tile_set, L_mm,
         L_read, exp_asked, exp_set, routed, up_mm, hid_act, hid_dve, down_mm, y_out, out_mm, scaled_set,
         summed, added, stored, pool_step) = room.sems(
            "step w_hi_set w_lo_set rstd_asked rstd n_set hi_set lo_set T_mm nTr_set tile_set L_mm "
            "L_read exp_asked exp_set routed up_mm hid_act hid_dve down_mm y_out out_mm scaled_set "
            "summed added stored pool_step")
        ident = early[:, ec["ident"]]

        def at(share):
            return int(share * UPG)
        OUT_AT = [OUT_FROM + k for k in range(T)]
        SCALE_AT = [u + 1 for u in OUT_AT]
        HI_AT, T_AT, NT_AT, TILE_AT, L_AT, ROUTE_AT = (9, 12, 14, 16, 17, 19) if layer == 0 else (7, 11, 12, 13, 14, 15)
        EXP_AT = UPG - 1
        END_AT = at(0.33)
        NORM_AT = ([0, 0, 1, 1, 2, 2] if layer == 0 else [0, 1, 2, 3]) + [OUT_FROM, LOW_AT]
        DOWN_LAG = 3
        Y_AT = [(k + 1) * CPP + DOWN_LAG + (Y_LATER if k == 0 else 0) for k in range(2 * PAIRS)]

        def chunk_of(u):
            pair, half, k = u // (2 * CPP), u // CPP % 2, u % CPP
            if layer == 0:
                return pair, half, 4 * pair + 2 * (k % 2) + k // 2
            return pair, half, 3 * pair + k

        def downs(u):
            pair, half, k = u // (2 * CPP), u // CPP % 2, u % CPP
            w = late[:, down_cols].rearrange("p (n d) -> p n d", d=D)
            if layer == 0:
                if k % 2 == 0:
                    return None
                j = k // 2
                return half, [(s, u - 1 + s, w[:, 4 * pair + 2 * s + j, :], j == 0, j == 1) for s in range(2)]
            if k == 0:
                return None
            if k == 1:
                return half, [(s, u - 1 + s, w[:, 4 * pair + s, :], True, False) for s in range(2)]
            return half, [(s, u, w[:, 4 * pair + 2 + s, :], False, True) for s in range(2)]

        def wait_hidden(eng, g, u):
            if layer == 1:
                need(eng, hid_dve, g * UPG + (u + 1))
            elif u % 2 == 0:
                need(eng, hid_act, g * (UPG // 2) + (u // 2 + 1))
            else:
                need(eng, hid_dve, g * (UPG // 2) + (u // 2 + 1))

        DOWNS_PER = 2

        def wait_ring(eng, g, u):
            v = u - HIDDEN_RING
            in_step = v % CPP // 2 + 1 if layer == 0 else (1, 1, 2)[v % CPP]
            need(eng, down_mm, g * (2 * PAIRS * DOWNS_PER) + (v // CPP * DOWNS_PER + in_step))

        act_taken, = room.sems("act_taken")
        with nc.Block() as block:
            @block.gpsimd
            def _(pool):
                chain = Chain(pool, pool_step)

                def deviation(g):
                    rstd_step(pool, stats, minus_half, rstd_asked, rstd, g + 1)

                def add_up(g):
                    pool.wait_ge(scaled_set, (g + 1) * T)
                    need(pool, added, g)
                    chain.link(pool.tensor_tensor(sum4[:, :, :], scaled[:, :, 0:4 * D], scaled[:, :, 4 * D:8 * D], ALU.add))
                    pool.sem_inc(summed, 1)
                    chain.link(pool.tensor_tensor(sum2[:, :, :], sum4[:, :, 0:2 * D], sum4[:, :, 2 * D:4 * D], ALU.add))
                    chain.link(pool.tensor_tensor(sum1[:, :, :], sum2[:, :, 0:D], sum2[:, :, D:2 * D], ALU.add))
                    tile = resid[:, bass.ds(g * T, T), :]
                    pool.tensor_tensor(tile, tile, sum1[:, :, :], ALU.add).then_inc(added, 1)
                    pool.wait_ge(added, g + 1)

                def exponentials(g):
                    if layer == 1:
                        pool.wait_ge(exp_asked, g + 1)
                        pool.tensor_tensor(small["prob"][:, :, :], base[:, :, :], small["d"][:, :, :], ALU.pow).then_inc(exp_set, 1)

                if layer == 1:
                    pool.memset(base[:, :, :], float(np.e)).then_inc(base_set, 1)
                    pool.wait_ge(base_set, 1)
                for g in range(2):
                    deviation(g)
                    exponentials(g)
                with pool.Fori(1, NT - 1) as g:
                    chain.enter(g - 1, 3)
                    deviation(g + 1)
                    add_up(g - 1)
                    exponentials(g + 1)
                chain.leave(NT - 2)
                for g in (NT - 2, NT - 1):
                    chain.enter(0, 3)
                    add_up(g)
                    chain.leave(1)

            @block.sync
            def _(sp):
                if layer == 1:
                    with sp.Fori(0, NT) as g:
                        sp.wait_ge(added, g + 1)
                        sp.dma_start(out[:, bass.ds(g * T, T), :], resid[:, bass.ds(g * T, T), :]).then_inc(stored, 16)
                    sp.wait_ge(stored, 16 * NT)

            @block.scalar
            def _(act):
                act.copy(w_hi[:, 0:NUP], late[:, up_cols]).then_inc(w_hi_set, 1)
                act.copy(w_hi[:, NUP:], late[:, gate_cols]).then_inc(w_hi_set, 1)

                def high_parts(g):
                    act.wait_ge(n_set, g + 1)
                    need(act, T_mm, g)
                    act.copy(split[:, :, 0:D].bitcast(F32R), nrm[:, :, :]).then_inc(hi_set, 1)

                def keep_transposed(g):
                    act.wait_ge(T_mm, g + 1)
                    take_waits(act, act_taken)
                    act.copy(tiles(nTr, g), psM[:, 0:TOK]).then_inc(nTr_set, 1)

                def exponentials(g):
                    if layer == 0:
                        act.wait_ge(exp_asked, g + 1)
                        act.activation(tiny["ex"][:, :], tiny["diff"][:, :], ACT.Exp).then_inc(exp_set, 1)

                def body(g, before, front):
                    for u in range(UPG):
                        if layer == 1 or u % 2 == 0:
                            act.wait_ge(up_mm, g * UPG + (u + 1))
                        if layer == 1:
                            need(act, hid_dve, g * UPG + (u - 3))
                            act.activation(sil[u % 4][:, :], psU[2 * (u % 2)][:, 0:HALF], ACT.Silu).then_inc(hid_act, 1)
                        elif u % 2 == 0:
                            wait_ring(act, g, u)
                            act.activation(hid[u % HIDDEN_RING][:, :], psU[u % 4][:, 0:HALF], ACT.Relu,
                                           bias=late[:, c["b1"]][:, chunk_of(u)[2]:chunk_of(u)[2] + 1]).then_inc(hid_act, 1)
                        for k, due in enumerate(Y_AT):
                            if due == u:
                                read_y(g, k)
                            elif before and due == u + UPG:
                                read_y(g - 1, k)
                        if front and u == HI_AT:
                            high_parts(g + 1)
                        if front and u == NT_AT:
                            keep_transposed(g + 1)
                        if front and u == EXP_AT:
                            exponentials(g + 1)

                def read_y(g, k):
                    pair, half = k // 2, k % 2
                    act.wait_ge(down_mm, (g * (2 * PAIRS) + (k + 1)) * DOWNS_PER)
                    need(act, out_mm, g * T)
                    dst = y[:, pair, half * HALF:(half + 1) * HALF]
                    if layer == 0:
                        ins = act.activation(dst, psY[half][:, 0:HALF], ACT.Identity, bias=late[:, c["b2"]][:, pair:pair + 1])
                    else:
                        ins = act.copy(dst, psY[half][:, 0:HALF])
                    ins.then_inc(y_out, 1)

                high_parts(0)
                keep_transposed(0)
                exponentials(0)
                body(0, False, True)
                with act.Fori(1, NT - 1) as g:
                    body(g, True, True)
                body(NT - 1, True, False)
                for k, due in enumerate(Y_AT):
                    if due >= UPG:
                        read_y(NT - 1, k)

            @block.vector
            def _(dve):
                chain = Chain(dve, step)
                dve.wait_ge(w_hi_set, 2)
                dve.tensor_tensor(w_lo[:, 0:NUP], late[:, up_cols], w_hi[:, 0:NUP].bitcast(F32), ALU.subtract).then_inc(w_lo_set, 1)
                dve.tensor_tensor(w_lo[:, NUP:], late[:, gate_cols], w_hi[:, NUP:].bitcast(F32), ALU.subtract).then_inc(w_lo_set, 1)

                def norm(g):
                    tile = src[:, bass.ds(g * T, T), :]
                    mean, var = stats[:, 0, :], stats[:, 1, :]
                    if layer == 0:
                        yield from chain.spread(dve.tensor_reduce(mean, tile, axis=AX.X, op=ALU.add))
                        yield from chain.spread(dve.tensor_scalar(mean, mean, 1.0 / D, None, ALU.mult))
                        yield from chain.spread(dve.tensor_tensor(cen[:, :, :], tile, over_width(mean), ALU.subtract))
                        tile = cen[:, :, :]
                    yield from chain.spread(dve.tensor_tensor(sq[:, :, :], tile, tile, ALU.mult))
                    yield from chain.spread(dve.tensor_reduce(var, sq[:, :, :], axis=AX.X, op=ALU.add))
                    dve.tensor_scalar(var, var, 1.0 / D, EPS_LN if layer == 0 else EPS_RMS, ALU.mult, ALU.add).then_inc(rstd_asked, 1)
                    yield
                    dve.wait_ge(rstd, g + 1)
                    rs = over_width(stats[:, 2, :])
                    if layer == 1:
                        yield from chain.spread(dve.tensor_tensor(cen[:, :, :], tile, rs, ALU.mult))
                        tile, rs = cen[:, :, :], late[:, c["ln2"]].unsqueeze(1).to_broadcast([B, T, D])
                    need(dve, lo_set, g)
                    dve.tensor_tensor(nrm[:, :, :], tile, rs, ALU.mult).then_inc(n_set, 1)
                    yield
                    dve.wait_ge(n_set, g + 1)
                    dve.wait_ge(hi_set, g + 1)
                    dve.tensor_tensor(split[:, :, D:], nrm[:, :, :], split[:, :, 0:D], ALU.subtract).then_inc(lo_set, 1)
                    yield

                NORM_STEPS = 5 if layer == 0 else 3
                descend = early[:, ec["descend"]].rearrange("b (t e) -> b t e", e=E)

                S = {k: v[:, :, :] for k, v in small.items()}
                V = {k: v[:, :] for k, v in tiny.items()}

                def over(x):
                    return x.unsqueeze(2).to_broadcast([B, T, E])

                def the_two():
                    return top_two(dve, chain, S["val"], (S["eq"], S["ranked"], S["left"], V["best"], S["first"],
                                   S["second"], V["m1"], V["m2"]), descend, 3e38 if layer == 0 else 3.0)

                def ask_routing(g):
                    logits = psM[:, TOK:TOK + T * E].rearrange("b (t e) -> b t e", e=E)
                    dve.wait_ge(L_mm, g + 1)
                    if layer == 0:
                        dve.tensor_tensor(S["val"], logits, late[:, c["gbias0"]].unsqueeze(1).to_broadcast([B, T, E]),
                                          ALU.add).then_inc(L_read, 1)
                        yield
                        dve.wait_ge(L_read, g + 1)
                    else:
                        yield from chain.spread(dve.tensor_reduce(V["m0"], logits, axis=AX.X, op=ALU.max))
                        dve.tensor_tensor(S["d"], logits, over(V["m0"]), ALU.subtract).then_inc(L_read, 1)
                        yield
                        dve.wait_ge(L_read, g + 1)
                        dve.sem_inc(exp_asked, 1)
                    if layer == 0:
                        yield from the_two()
                        dve.tensor_tensor(V["diff"], V["m2"], V["m1"], ALU.subtract).then_inc(exp_asked, 1)

                def end_routing(g):
                    dst = weights[:, bass.ds(g * T, T), :]
                    dve.wait_ge(exp_set, g + 1)
                    if layer == 0:
                        yield from chain.spread(dve.tensor_scalar(V["den"], V["ex"], 1.0, None, ALU.add))
                        yield from chain.spread(dve.reciprocal(V["rec"], V["den"]))
                        yield from chain.spread(dve.tensor_tensor(V["w2"], V["ex"], V["rec"], ALU.mult))
                        one, two = V["rec"], V["w2"]
                    else:
                        yield from chain.spread(dve.tensor_reduce(V["sum"], S["prob"], axis=AX.X, op=ALU.add))
                        yield from chain.spread(dve.reciprocal(V["rec"], V["sum"]))
                        yield from chain.spread(dve.tensor_tensor(S["val"], S["prob"], over(V["rec"]), ALU.mult))
                        yield from the_two()
                        yield from chain.spread(dve.tensor_tensor(V["den"], V["m1"], V["m2"], ALU.add))
                        yield from chain.spread(dve.tensor_scalar(V["den"], V["den"], 1e-9, None, ALU.add))
                        yield from chain.spread(dve.reciprocal(V["rec"], V["den"]))
                        one, two = V["m1"], V["m2"]
                    yield from chain.spread(dve.tensor_tensor(S["first"], S["first"], over(one), ALU.mult))
                    yield from chain.spread(dve.tensor_tensor(S["second"], S["second"], over(two), ALU.mult))
                    if layer == 0:
                        dve.tensor_tensor(dst, S["first"], S["second"], ALU.add).then_inc(routed, 1)
                    else:
                        yield from chain.spread(dve.tensor_tensor(S["a"], S["first"], S["second"], ALU.add))
                        dve.tensor_tensor(dst, S["a"], over(V["rec"]), ALU.mult).then_inc(routed, 1)
                    yield
                    dve.wait_ge(routed, g + 1)

                ASK_STEPS, END_STEPS = (TOP_TWO_LINKS, 5) if layer == 0 else (1, TOP_TWO_LINKS + 9)

                def stationary(g):
                    dve.wait_ge(nTr_set, g + 1)
                    need(dve, L_mm, g)
                    dve.tensor_copy(nT_tile[:, :], tiles(nTr, g).bitcast(F32)).then_inc(tile_set, 1)

                def weigh(g, t):
                    dve.wait_ge(out_mm, g * T + (t + 1))
                    if t == 0:
                        need(dve, summed, g)
                    dve.tensor_tensor(scaled[:, t, :].rearrange("b (e d) -> b e d", e=E),
                                      psM[:, 512 * (t % 2):512 * (t % 2) + E * D].rearrange("b (e d) -> b e d", e=E),
                                      weights[:, bass.ds(g * T + t, 1), :].squeeze(1).unsqueeze(2).to_broadcast([B, E, D]),
                                      ALU.mult).then_inc(scaled_set, 1)

                def body(g, before, front):
                    n, ask, end = norm(g + 1), ask_routing(g + 1), end_routing(g)
                    for u in range(UPG):
                        if before and u in SCALE_AT:
                            weigh(g - 1, SCALE_AT.index(u))
                        if layer == 1:
                            dve.wait_ge(hid_act, g * UPG + (u + 1))
                            wait_ring(dve, g, u)
                            dve.tensor_tensor(hid[u % HIDDEN_RING][:, :], psU[2 * (u % 2) + 1][:, 0:HALF], sil[u % 4][:, :],
                                              ALU.mult).then_inc(hid_dve, 1)
                        elif u % 2 == 1:
                            dve.wait_ge(up_mm, g * UPG + (u + 1))
                            wait_ring(dve, g, u)
                            k = chunk_of(u)[2]
                            dve.tensor_scalar(hid[u % HIDDEN_RING][:, :], psU[u % 4][:, 0:HALF], late[:, c["b1"]][:, k:k + 1],
                                              0.0, ALU.add, ALU.max).then_inc(hid_dve, 1)
                        if front and u == TILE_AT:
                            stationary(g + 1)
                        if front:
                            for _ in range(NORM_AT.count(u)):
                                next(n, None)
                        if front and u >= ROUTE_AT:
                            next(ask, None), next(ask, None)
                        if u >= END_AT:
                            next(end, None), next(end, None)
                    if front:
                        for _ in n:
                            pass
                        for _ in ask:
                            pass
                    for _ in end:
                        pass

                chain.enter(0, NORM_STEPS + ASK_STEPS)
                for _ in norm(0):
                    pass
                stationary(0)
                for _ in ask_routing(0):
                    pass
                chain.leave(1)
                chain.enter(0, NORM_STEPS + ASK_STEPS + END_STEPS)
                body(0, False, True)
                chain.leave(1)
                with dve.Fori(1, NT - 1) as g:
                    chain.enter(g - 1, NORM_STEPS + ASK_STEPS + END_STEPS)
                    body(g, True, True)
                chain.leave(NT - 2)
                chain.enter(0, END_STEPS)
                body(NT - 1, True, False)
                chain.leave(1)
                for t in range(T):
                    weigh(NT - 1, t)

            @block.tensor
            def _(pe):
                def transposes(g):
                    pe.wait_ge(lo_set, g + 1)
                    need(pe, scaled_set, (g - 1) * T)
                    need(pe, L_read, g)
                    for t in range(T):
                        last = pe.transpose(psM[:, t * B:(t + 1) * B], split[:, t, :], ident)
                    last.then_inc(T_mm, 1)

                def logits(g):
                    pe.wait_ge(tile_set, g + 1)
                    for t in range(T):
                        for part, w in enumerate((w_hi, w_lo)):
                            last = pe.matmul(psM[:, TOK + t * E:TOK + (t + 1) * E], nT_tile[:, t * B:(t + 1) * B], w[:, NUP:],
                                             start=(part == 0), stop=(part == 1))
                    last.then_inc(L_mm, 1)

                def up(g, u):
                    _, half, chunk = chunk_of(u)
                    kinds = 1 + layer
                    if layer == 0:
                        wait_psum = u - 4
                    else:
                        wait_psum = u - 2
                    wait_hidden(pe, g, wait_psum)
                    for kind in range(kinds):
                        dst = psU[u % 4 if layer == 0 else 2 * (u % 2) + kind][:, 0:HALF]
                        col = (kind * CH1 + chunk) * SPLIT
                        for part, w in enumerate((w_hi, w_lo)):
                            last = pe.matmul(dst, w[:, col:col + SPLIT], nTr[:, bass.ds(g * TOK + half * HALF, HALF)],
                                             start=(part == 0), stop=(part == 1))
                    last.then_inc(up_mm, 1)

                def down(g, u):
                    due = downs(u)
                    if due is None:
                        return
                    half, parts = due
                    k = u // CPP
                    if parts[0][3]:
                        need(pe, y_out, g * (2 * PAIRS) + (k - 1))
                    if layer == 0:
                        wait_hidden(pe, g, parts[0][1])
                    wait_hidden(pe, g, parts[1][1])
                    for side, v, w, start, stop in parts:
                        last = pe.matmul(psY[half][64 * side:64 * side + 64, 0:HALF], w, hid[v % HIDDEN_RING][:, :],
                                         start=start, stop=stop)
                    last.then_inc(down_mm, 1)

                def token_major(g, t):
                    need(pe, y_out, (g + 1) * (2 * PAIRS))
                    need(pe, scaled_set, g * T + max(t - 1, 0))
                    for pair in range(PAIRS):
                        last = pe.transpose(psM[:, 512 * (t % 2) + pair * 128:512 * (t % 2) + (pair + 1) * 128],
                                            y[:, pair, t * B:(t + 1) * B], ident)
                    last.then_inc(out_mm, 1)

                def body(g, before, front):
                    for u in range(UPG):
                        up(g, u)
                        if u >= DOWN_LAG:
                            down(g, u - DOWN_LAG)
                        elif before:
                            down(g - 1, UPG + u - DOWN_LAG)
                        if before and u in OUT_AT:
                            if u == OUT_AT[0]:
                                need(pe, L_read, g + 1)
                            token_major(g - 1, OUT_AT.index(u))
                        if front and u == T_AT:
                            transposes(g + 1)
                        if front and u == L_AT:
                            logits(g + 1)

                pe.wait_ge(w_lo_set, 2)
                transposes(0)
                logits(0)
                body(0, False, True)
                with pe.Fori(1, NT - 1) as g:
                    body(g, True, True)
                body(NT - 1, True, False)
                for u in range(UPG - DOWN_LAG, UPG):
                    down(NT - 1, u)
                need(pe, L_read, NT)
                for t in range(T):
                    token_major(NT - 1, t)


def recurrence(nc, late, early, h, minus_half):
    c, ec = columns(LATE)[0], columns(EARLY)[0]
    with ExitStack() as ctx:
        room = Room(nc, ctx, "recur")
        sb, ps = room.sb, room.ps
        lam, in_w, out_w = sb("lambda", [128, 128]), sb("in_w", [64, 128]), sb("out_w", [128, D])
        modulus, theta = sb("modulus", [128, 1]), sb("theta", [128, 1])
        ang, turns, trig = sb("ang", [128, 2]), sb("turns", [128, 2]), sb("trig", [128, 2])
        lam_part = sb("lambda_part", [128, 128])
        n_tile, nT = sb("n_tile", [B, T, D]), sb("nT", [D, L * B])
        cen, sq, stats = sb("cen", [B, T, D]), sb("sq", [B, T, D]), sb("stats", [B, 3, T])
        s = sb("state", [128, T, B])
        psT, psY = ps("psT", D, TOK), ps("psY", B, T * D)
        psS = [ps(f"psS{k}", 128, B) for k in range(2)]
        (step, exps, ang_set, trig_set, tables, rstd_asked, rstd, n_set, T_mm, nT_set, S_mm, s_set, Y_mm, added, taken) = \
            room.sems("step exps ang_set trig_set tables rstd_asked rstd n_set T_mm nT_set S_mm s_set Y_mm added taken")
        ident = early[:, ec["ident"]]
        with nc.Block() as block:
            @block.gpsimd
            def _(pool):
                with pool.Fori(0, NT) as g:
                    rstd_step(pool, stats, minus_half, rstd_asked, rstd, g + 1)

            @block.scalar
            def _(act):
                act.activation(modulus[:, :], late[:, c["nu"]], ACT.Exp).then_inc(exps, 1)
                act.wait_ge(exps, 1)
                act.activation(modulus[:, :], modulus[:, :], ACT.Exp, scale=-1.0).then_inc(exps, 1)
                act.activation(theta[:, :], late[:, c["theta"]], ACT.Exp).then_inc(exps, 1)
                act.activation(in_w[:, :], late[0:64, c["gamma"]], ACT.Exp).then_inc(exps, 1)
                act.wait_ge(ang_set, 1)
                act.activation(trig[:, :], ang[:, :], ACT.Sin).then_inc(trig_set, 1)
                with act.Fori(0, NT) as g:
                    for t in range(T):
                        act.wait_ge(S_mm, g * T + (t + 1))
                        act.copy(s[:, t, :], psS[t % 2][:, 0:B]).then_inc(s_set, 1)

            @block.tensor
            def _(pe):
                def transposes(g):
                    pe.wait_ge(n_set, g + 1)
                    need(pe, nT_set, g)
                    take_waits(pe, taken)
                    for t in range(T):
                        last = pe.transpose(psT[:, t * B:(t + 1) * B], n_tile[:, t, :], ident)
                    last.then_inc(T_mm, 1)

                def enter(g, t):
                    pe.matmul(psS[t % 2][:, 0:B], in_w[:, :], nT[:, bass.ds(g * TOK + t * B, B)], start=True, stop=False)

                def states(g, more):
                    pe.wait_ge(nT_set, g + 1)
                    need(pe, s_set, g * T)
                    take_waits(pe, taken)
                    enter(g, 0)
                    for t in range(T):
                        need(pe, s_set, g * T + t)
                        pe.matmul(psS[t % 2][:, 0:B], lam[:, :], s[:, (t - 1) % T, :], start=False, stop=True).then_inc(S_mm, 1)
                        if t < T - 1:
                            enter(g, t + 1)
                        if t == 0:
                            need(pe, added, g)
                        else:
                            output(t - 1)
                        if more and t == 1:
                            transposes(g + 1)
                    pe.wait_ge(s_set, g * T + T)
                    output(T - 1).then_inc(Y_mm, 1)

                def output(t):
                    return pe.matmul(psY[:, t * D:(t + 1) * D], s[:, t, :], out_w[:, :], start=True, stop=True)

                transposes(0)
                pe.wait_ge(tables, 3)
                with pe.Fori(0, NT - 1) as g:
                    states(g, True)
                states(NT - 1, False)

            @block.vector
            def _(dve):
                chain = Chain(dve, step)

                def norm(g, meanwhile=None):
                    norm_statistics(dve, chain, h[:, bass.ds(g * T, T), :], cen[:, :, :], sq[:, :, :], stats, rstd_asked)
                    if meanwhile is not None:
                        meanwhile()
                    dve.wait_ge(rstd, g + 1)
                    need(dve, T_mm, g)
                    dve.tensor_tensor(n_tile[:, :, :], cen[:, :, :], over_width(stats[:, 2, :]), ALU.mult).then_inc(n_set, 1)

                def keep_transposed(g):
                    dve.wait_ge(T_mm, g + 1)
                    dve.tensor_copy(tiles(nT, g), psT[:, 0:TOK]).then_inc(nT_set, 1)

                def residual(g):
                    dve.wait_ge(Y_mm, g + 1)
                    tile = h[:, bass.ds(g * T, T), :].rearrange("b t d -> b (t d)")
                    dve.tensor_tensor(tile, tile, psY[:, 0:T * D], ALU.add).then_inc(added, 1)

                dve.wait_ge(exps, 4)
                chain.link(dve.tensor_copy(ang[:, 0:1], theta[:, :]))
                chain.link(dve.tensor_copy(ang[:, 1:2], theta[:, :]))
                reduced_angle(dve, chain, ang[:, 0:1], turns[:, 0:1], 0.0, 0.0)
                reduced_angle(dve, chain, ang[:, 1:2], turns[:, 1:2], 0.25, PI / 2)
                dve.sem_inc(ang_set, 1)
                dve.tensor_tensor(in_w[:, :], in_w[:, :], late[0:64, c["bT"]], ALU.mult).then_inc(tables, 1)
                dve.tensor_scalar(out_w[:, :], late[:, c["cT"]], late[:, c["c_sign"]], None, ALU.mult).then_inc(tables, 1)
                chain.link(dve.memset(s[:, T - 1, :], 0.0))
                dve.wait_ge(trig_set, 1)
                chain.link(dve.tensor_tensor(trig[:, :], trig[:, :], modulus[:, 0:1].to_broadcast([128, 2]), ALU.mult))
                chain.link(dve.tensor_scalar(lam_part[:, :], late[:, c["rotJ"]], trig[:, 0:1], None, ALU.mult))
                dve.scalar_tensor_tensor(lam[:, :], ident, trig[:, 1:2], lam_part[:, :], ALU.mult, ALU.add).then_inc(tables, 1)
                chain.leave_straight()
                for g in range(2):
                    chain.enter(0, NORM_LINKS)
                    norm(g)
                    chain.leave(1)
                    if g == 0:
                        keep_transposed(0)
                with dve.Fori(0, NT - 2) as g:
                    chain.enter(g, NORM_LINKS)
                    keep_transposed(g + 1)
                    norm(g + 2, lambda: residual(g))
                chain.leave(NT - 2)
                keep_transposed(NT - 1)
                residual(NT - 2)
                residual(NT - 1)


def attention1(nc, late, early, h, x, minus_half):
    with ExitStack() as ctx:
        sb = Room(nc, ctx, "attention1").sb
        nT, qx, kx = sb("nT", [D, L * B]), sb("queries", [128, L * B]), sb("keys", [128, L * B])
        project1(nc, late, early, h, x, minus_half, nT, qx, kx)
        heads1(nc, late, early, nT, qx, kx)
        output1(nc, late, h, x, nT)


def project1(nc, late, early, h, x, minus_half, nT, qx, kx):
    c, ec = columns(LATE)[0], columns(EARLY)[0]
    with ExitStack() as ctx:
        room = Room(nc, ctx, "project1")
        sb, ps = room.sb, room.ps
        cen, sq, stats = sb("cen", [B, T, D]), sb("sq", [B, T, D]), sb("stats", [B, 3, T])
        stats2, n_tile, k_parts = sb("stats2", [B, 3, T]), sb("n_tile", [B, T, D]), sb("k_parts", [128, TOK])
        psT, psQ, psK, psF = ps("psT", D, TOK), ps("psQ", 128, TOK), ps("psK", 128, TOK), ps("psF", 128, TOK)
        (step, rstd_asked, rstd, x_set, rms_asked, rms, n_set, T_mm, nT_set, Q_mm, q_set, K_mm, k_parts_set, F_mm, k_set, taken) = \
            room.sems("step rstd_asked rstd x_set rms_asked rms n_set T_mm nT_set Q_mm q_set K_mm k_parts_set F_mm k_set taken")
        act_taken, = room.sems("act_taken")
        with nc.Block() as block:
            @block.gpsimd
            def _(pool):
                with pool.Fori(0, NT) as g:
                    rstd_step(pool, stats, minus_half, rstd_asked, rstd, g + 1)
                    rstd_step(pool, stats2, minus_half, rms_asked, rms, g + 1)

            @block.vector
            def _(dve):
                chain = Chain(dve, step)

                def norm(g, during_rstd=None, during_rms=None):
                    tile = bass.ds(g * T, T)
                    norm_statistics(dve, chain, h[:, tile, :], cen[:, :, :], sq[:, :, :], stats, rstd_asked)
                    if during_rstd is not None:
                        during_rstd()
                    dve.wait_ge(rstd, g + 1)
                    dve.tensor_tensor(x[:, tile, :], cen[:, :, :], over_width(stats[:, 2, :]), ALU.mult).then_inc(x_set, 1)
                    dve.wait_ge(x_set, g + 1)
                    chain.link(dve.tensor_tensor(sq[:, :, :], x[:, tile, :], x[:, tile, :], ALU.mult))
                    chain.link(dve.tensor_reduce(stats2[:, 1, :], sq[:, :, :], axis=AX.X, op=ALU.add))
                    dve.tensor_scalar(stats2[:, 1, :], stats2[:, 1, :], 1.0 / D, EPS_RMS, ALU.mult, ALU.add).then_inc(rms_asked, 1)
                    if during_rms is not None:
                        during_rms()
                    dve.wait_ge(rms, g + 1)
                    need(dve, T_mm, g)
                    dve.tensor_tensor(n_tile[:, :, :], x[:, tile, :], over_width(stats2[:, 2, :]), ALU.mult).then_inc(n_set, 1)

                def rotate(g, mm, src, table, dst, done):
                    dve.wait_ge(mm, g + 1)
                    if done is k_parts_set:
                        need(dve, F_mm, g)
                    angles = late[:, c[table]][:, bass.ds(g * T, T)].unsqueeze(2).to_broadcast([128, T, B])
                    dve.tensor_tensor(dst.rearrange("p (t b) -> p t b", b=B),
                                      src[:, 0:TOK].rearrange("p (t b) -> p t b", b=B), angles, ALU.mult).then_inc(done, 1)

                def keys(g):
                    rotate(g, K_mm, psK, "ropek", k_parts[:, :], k_parts_set)

                def queries(g):
                    rotate(g, Q_mm, psQ, "ropeq", tiles(qx, g), q_set)

                for g in range(2):
                    chain.enter(0, NORM_LINKS + 2)
                    norm(g)
                    chain.leave(1)
                with dve.Fori(0, NT - 2) as g:
                    chain.enter(g, NORM_LINKS + 2)
                    norm(g + 2, lambda: keys(g), lambda: queries(g))
                chain.leave(NT - 2)
                for g in range(NT - 2, NT):
                    keys(g)
                    queries(g)

            @block.scalar
            def _(act):
                def transposed(g):
                    act.wait_ge(T_mm, g + 1)
                    take_waits(act, act_taken)
                    act.activation(tiles(nT, g), psT[:, 0:TOK], ACT.Copy, scale=late[0:D, c["ln1"]]).then_inc(nT_set, 1)

                def folded(g):
                    act.wait_ge(F_mm, g + 1)
                    take_waits(act, act_taken)
                    act.copy(tiles(kx, g), psF[:, 0:TOK]).then_inc(k_set, 1)

                transposed(0)
                with act.Fori(0, NT - 1) as g:
                    transposed(g + 1)
                    folded(g)
                folded(NT - 1)

            @block.tensor
            def _(pe):
                def transposes(g):
                    pe.wait_ge(n_set, g + 1)
                    need(pe, nT_set, g)
                    take_waits(pe, taken)
                    for t in range(T):
                        last = pe.transpose(psT[:, t * B:(t + 1) * B], n_tile[:, t, :], early[:, ec["ident"]])
                    last.then_inc(T_mm, 1)

                def product(g, psum, w, read, done):
                    pe.wait_ge(nT_set, g + 1)
                    need(pe, read, g)
                    take_waits(pe, taken)
                    for at, n in pieces():
                        last = pe.matmul(psum[:, at:at + n], late[0:D, c[w]], nT[:, bass.ds(g * TOK + at, n)],
                                         start=True, stop=True)
                    last.then_inc(done, 1)

                def fold(g):
                    pe.wait_ge(k_parts_set, g + 1)
                    need(pe, k_set, g)
                    for at, n in pieces():
                        last = pe.matmul(psF[:, at:at + n], late[:, c["fold"]], k_parts[:, at:at + n], start=True, stop=True)
                    last.then_inc(F_mm, 1)

                def step(g, more):
                    product(g, psK, "wkx", k_parts_set, K_mm)
                    if more:
                        transposes(g + 1)
                    product(g, psQ, "wqx", q_set, Q_mm)
                    fold(g)

                transposes(0)
                with pe.Fori(0, NT - 1) as g:
                    step(g, True)
                step(NT - 1, False)


def heads1(nc, late, early, nT, qx, kx):
    c, ec = columns(LATE)[0], columns(EARLY)[0]
    BF16 = mybir.dt.bfloat16
    NP = BG // 2
    HL = NH * L
    KP = 128
    with ExitStack() as ctx:
        room = Room(nc, ctx, "heads1")
        sb, ps = room.sb, room.ps
        qb, kb = sb("queries_b", [128, BG, L]), sb("keys_b", [128, BG, NH, L])
        nTb = sb("nT_b", [D, BG, L])
        val = sb("values", [KP, BG, 2, HD + 1])
        fresh = sb("fresh", [L, BG * 2 * HD])
        prob = [sb(f"prob{k}", [KP, 2 * NH, L]) for k in range(2)]
        probT = [sb(f"probT{k}", [KP, 2 * NH, L]) for k in range(2)]
        top = [sb(f"top{k}", [L, 2 * NH]) for k in range(2)]
        inv, yb = sb("inv", [L, BG // 2 * NH]), sb("y_b", [L, BG // 2, D])
        mask, unit = sb("mask", [L, NH, L], BF16), sb("unit", [L, L], BF16)
        psS = [ps(f"psS{k}", L, 1024)[:, :].rearrange("t (b n) -> t b n", b=2)[:, :, 0:HL] for k in range(2)]
        turned = ps("psP", L, 1024)[:, :].rearrange("s (b n) -> s b n", b=2)
        psP, psVal = turned[:, :, 0:HL], turned[:, :, 512 - BG // 2 * 32:]
        psY, psO = ps("psY", L, 512), ps("psO", L, 512)
        (consts, zeroed, padded, pool_taken, fresh_set, nTb_set, qb_set, kb_set, V_mm, val_set, S_mm, top_set, sub_set, exp_set, P_mm, pT_set, O_mm, inv_set, yb_set,
         Y_mm, y_set, taken) = room.sems("consts zeroed padded pool_taken fresh_set nTb_set qb_set kb_set V_mm val_set S_mm top_set sub_set exp_set P_mm pT_set O_mm "
                                  "inv_set yb_set Y_mm y_set taken")

        def batches(t, i, rows):
            return t[rows, :].rearrange("p (t b) -> p b t", b=B)[:, bass.ds(i * BG, BG), :]

        act_taken, = room.sems("act_taken")
        with nc.Block() as block:
            @block.gpsimd
            def _(pool):
                pool.memset(kb[:, :, :, :], 0.0).then_inc(zeroed, 1)
                pool.wait_ge(zeroed, 1)
                for a in prob + probT:
                    ins = pool.memset(a[64:KP, :, :], 0.0)
                ins.then_inc(padded, 1)
                pool.wait_ge(padded, 1)
                pool.memset(val[:, :, :, :], 1.0).then_inc(consts, 1)
                pool.wait_ge(consts, 3)

                def values_in_place(i):
                    pool.wait_ge(fresh_set, i + 1)
                    need(pool, O_mm, i * NP)
                    take_waits(pool, pool_taken)
                    pool.tensor_copy(val[0:L, :, :, 0:HD].rearrange("s b g d -> s (b g) d"),
                                     fresh[:, :].rearrange("s (n d) -> s n d", d=HD)).then_inc(val_set, 1)

                with pool.Fori(0, NBG) as i:
                    values_in_place(i)

            @block.tensor
            def _(pe):
                def values_projected(i):
                    pe.wait_ge(nTb_set, i + 1)
                    take_waits(pe, taken)
                    for b in range(BG):
                        last = pe.matmul(psVal[:, b // (BG // 2), (b % (BG // 2)) * 32:(b % (BG // 2) + 1) * 32], nTb[:, b, :],
                                         late[0:D, c["wv"]], start=True, stop=True)
                    last.then_inc(V_mm, 1)

                def scores(i, k):
                    if k % NP == 0:
                        pe.wait_ge(qb_set, i + (k // NP + 1))
                        pe.wait_ge(kb_set, i * 2 + (k // NP * 2 + 1))
                    if k % NP == NP // 2:
                        pe.wait_ge(kb_set, i * 2 + (k // NP * 2 + 2))
                    if k >= 2:
                        pe.wait_ge(sub_set, i * NP + (k - 1))
                    for j in range(2):
                        pe.matmul(psS[k % 2][:, j, :], unit[:, :], mask[:, :, :].rearrange("t h s -> t (h s)"),
                                  start=True, stop=False)
                        b = 2 * (k % NP) + j
                        last = pe.matmul(psS[k % 2][:, j, :], qb[:, b, :],
                                         kb[:, b, :, :].rearrange("p h s -> p (h s)"), start=False, stop=True)
                    last.then_inc(S_mm, 1)

                def turn(i, k, more=False):
                    pe.wait_ge(exp_set, i * NP + (k + 1))
                    need(pe, pT_set, i * NP + k)
                    if k == NP - 1:
                        need(pe, fresh_set, i + 2 if more else 0)
                    for n in range(2 * NH):
                        last = pe.matmul(psP[:, n // NH, (n % NH) * L:(n % NH + 1) * L], prob[k % 2][:, n, :],
                                         early[0:KP, ec["ident"]][:, 0:L], start=True, stop=True)
                    last.then_inc(P_mm, 1)

                def values(i, k):
                    pe.wait_ge(pT_set, i * NP + (k + 1))
                    if k == 0:
                        pe.wait_ge(val_set, i + 1)
                    if k % 2 == 0:
                        need(pe, yb_set, i * 2 + k // 2)
                    for n in range(2 * NH):
                        b, hd = 2 * k + n // NH, n % NH
                        at = (b % (BG // 2) * NH + hd) * (HD + 1)
                        last = pe.matmul(psO[:, at:at + HD + 1], probT[k % 2][:, n, :], val[:, b, hd // 2, :],
                                         start=True, stop=True)
                    last.then_inc(O_mm, 1)

                def outputs(i, half):
                    pe.wait_ge(yb_set, i * 2 + (half + 1))
                    need(pe, y_set, i * 2 + half)
                    take_waits(pe, taken)
                    for b in range(BG // 2):
                        last = pe.transpose(psY[0:D, b * L:(b + 1) * L], yb[:, b, :], early[0:L, ec["ident"]][:, 0:L])
                    last.then_inc(Y_mm, 1)

                def step(i, more):
                    values(i, 0)
                    turn(i, 1)
                    scores(i, 3)
                    values(i, 1)
                    turn(i, 2)
                    if more:
                        scores(i, NP)
                        pe.wait_ge(pT_set, i * NP + NP - 1)
                        values_projected(i + 1)
                    values(i, 2)
                    turn(i, 3, more)
                    outputs(i, 0)
                    if more:
                        scores(i, NP + 1)
                    values(i, 3)
                    if more:
                        turn(i, NP)
                        scores(i, NP + 2)
                    outputs(i, 1)

                pe.wait_ge(consts, 3)
                pe.wait_ge(padded, 1)
                values_projected(0)
                scores(0, 0)
                scores(0, 1)
                pe.wait_ge(fresh_set, 1)
                turn(0, 0)
                scores(0, 2)
                with pe.Fori(0, NBG - 1) as i:
                    step(i, True)
                step(NBG - 1, False)

            @block.vector
            def _(dve):
                def keys(i, half):
                    need(dve, S_mm, (i - 1) * NP + (half + 1) * NP // 2)
                    own = slice(half * BG // 2, (half + 1) * BG // 2)
                    for hd in range(NH):
                        rows = slice(32 * hd, 32 * hd + 32)
                        src = kx[rows, :].rearrange("p (t b) -> p t b", b=B)[:, :, bass.ds(i * BG + half * (BG // 2), BG // 2)]
                        ins = dve.tensor_copy(kb[rows, own, hd, :].rearrange("p b t -> p t b"), src)
                    ins.then_inc(kb_set, 1)

                def less_maximum(i, k):
                    dve.wait_ge(S_mm, i * NP + (k + 1))
                    view = psS[k % 2].rearrange("t b (h s) -> t b h s", s=L)
                    out4 = prob[k % 2][0:L, :, :].rearrange("t (b h) s -> t b h s", b=2)
                    if k >= 2:
                        dve.wait_ge(P_mm, i * NP + (k - 1))
                    dve.tensor_reduce(top[k % 2][:, :].rearrange("t (b h) -> t b h", b=2), view, axis=AX.X,
                                      op=ALU.max).then_inc(top_set, 1)
                    dve.wait_ge(top_set, i * NP + (k + 1))
                    for j in range(2):
                        ins = dve.tensor_tensor(out4[:, j], view[:, j],
                                                top[k % 2][:, j * NH:(j + 1) * NH].unsqueeze(2).to_broadcast([L, NH, L]),
                                                ALU.subtract)
                    ins.then_inc(sub_set, 1)

                def step(i, more):
                    if more:
                        keys(i + 1, 0)
                    less_maximum(i, 3)
                    divide(dve, i, 0, psO, inv, yb, O_mm, inv_set, yb_set, Y_mm, NP)
                    if more:
                        keys(i + 1, 1)
                    if more:
                        less_maximum(i, NP)
                        less_maximum(i, NP + 1)
                    divide(dve, i, 1, psO, inv, yb, O_mm, inv_set, yb_set, Y_mm, NP)
                    if more:
                        less_maximum(i, NP + 2)

                dve.tensor_copy(mask[:, :, :], late[0:L, c["mask1"]].unsqueeze(1).to_broadcast([L, NH, L])).then_inc(consts, 1)
                dve.tensor_copy(unit[:, :], early[0:L, ec["ident"]][:, 0:L]).then_inc(consts, 1)
                dve.wait_ge(zeroed, 1)
                dve.wait_ge(padded, 1)
                keys(0, 0)
                keys(0, 1)
                less_maximum(0, 0)
                less_maximum(0, 1)
                less_maximum(0, 2)
                with dve.Fori(0, NBG - 1) as i:
                    step(i, True)
                step(NBG - 1, False)

            @block.scalar
            def _(act):
                def transposed_norm(i):
                    need(act, V_mm, i)
                    take_waits(act, act_taken)
                    act.copy(nTb[:, :, :].rearrange("p b t -> p t b"),
                             batches(nT, i, slice(0, D)).rearrange("p b t -> p t b")).then_inc(nTb_set, 1)

                def queries(i):
                    need(act, S_mm, i * NP)
                    take_waits(act, act_taken)
                    act.copy(qb[:, :, :].rearrange("p b t -> p t b"),
                             batches(qx, i, slice(0, 128)).rearrange("p b t -> p t b")).then_inc(qb_set, 1)

                def keep_values(i):
                    act.wait_ge(V_mm, i + 1)
                    need(act, val_set, i)
                    act.copy(fresh[:, :].rearrange("s (x n) -> s x n", x=2), psVal).then_inc(fresh_set, 1)

                def exponential(i, k):
                    act.wait_ge(sub_set, i * NP + (k + 1))
                    act.activation(prob[k % 2][0:L, :, :], prob[k % 2][0:L, :, :], ACT.Exp).then_inc(exp_set, 1)

                def keep_turned(i, k):
                    act.wait_ge(P_mm, i * NP + (k + 1))
                    need(act, O_mm, i * NP + (k - 1)) if k >= 2 else need(act, O_mm, i * NP)
                    act.copy(probT[k % 2][0:L, :, :].rearrange("s (b h) t -> s b (h t)", b=2), psP).then_inc(pT_set, 1)

                def keep_outputs(i, half):
                    act.wait_ge(Y_mm, i * 2 + (half + 1))
                    dst = nT[:, :].rearrange("p (t b) -> p b t", b=B)[:, bass.ds(i * BG + half * (BG // 2), BG // 2), :]
                    take_waits(act, act_taken)
                    act.copy(dst, psY[0:D, 0:BG // 2 * L].rearrange("d (b t) -> d b t", t=L)).then_inc(y_set, 1)

                def step(i, more):
                    keep_turned(i, 1)
                    if more:
                        transposed_norm(i + 1)
                    exponential(i, 3)
                    if more:
                        queries(i + 1)
                    keep_turned(i, 2)
                    if more:
                        keep_values(i + 1)
                        exponential(i, NP)
                    keep_turned(i, 3)
                    keep_outputs(i, 0)
                    if more:
                        exponential(i, NP + 1)
                        keep_turned(i, NP)
                        exponential(i, NP + 2)
                    keep_outputs(i, 1)

                act.wait_ge(consts, 3)
                transposed_norm(0)
                queries(0)
                keep_values(0)
                exponential(0, 0)
                exponential(0, 1)
                keep_turned(0, 0)
                exponential(0, 2)
                with act.Fori(0, NBG - 1) as i:
                    step(i, True)
                step(NBG - 1, False)


def divide(dve, i, half, psO, inv, yb, O_mm, inv_set, yb_set, Y_mm, NP):
    dve.wait_ge(O_mm, i * NP + 2 * (half + 1))
    heads = psO[:, 0:BG // 2 * NH * (HD + 1)].rearrange("t (n d) -> t n d", d=HD + 1)
    dve.reciprocal(inv[:, :], heads[:, :, HD:HD + 1].squeeze(2)).then_inc(inv_set, 1)
    dve.wait_ge(inv_set, i * 2 + (half + 1))
    need(dve, Y_mm, i * 2 + half)
    dve.tensor_tensor(yb[:, :, :].rearrange("t b (h d) -> t (b h) d", d=HD), heads[:, :, 0:HD],
                      inv[:, :].unsqueeze(2).to_broadcast([L, BG // 2 * NH, HD]), ALU.mult).then_inc(yb_set, 1)


def output1(nc, late, h, x, yT):
    c, _ = columns(LATE)
    with ExitStack() as ctx:
        room = Room(nc, ctx, "output1")
        y_tile = [room.sb(f"y_tile{k}", [D, TOK]) for k in range(2)]
        psW = [room.ps(f"psW{k}", B, T * D) for k in range(2)]
        staged, W_mm, x_set, h_set = room.sems("staged W_mm x_set h_set")
        act_taken, = room.sems("act_taken")

        def over_tiles(eng, step):
            step(0, 0)
            step(1, 1)
            with eng.Fori(1, NT // 2) as n:
                step(n * 2, 0)
                step(n * 2 + 1, 1)
            step(NT - 1, 0)

        with nc.Block() as block:
            @block.scalar
            def _(act):
                def stage(g, k):
                    need(act, W_mm, g - 1)
                    take_waits(act, act_taken)
                    act.copy(y_tile[k][:, :], tiles(yT, g)).then_inc(staged, 1)

                over_tiles(act, stage)

            @block.tensor
            def _(pe):
                def project(g, k):
                    pe.wait_ge(staged, g + 1)
                    need(pe, x_set, g - 1)
                    for t in range(T):
                        last = pe.matmul(psW[k][:, t * D:(t + 1) * D], y_tile[k][:, t * B:(t + 1) * B], late[0:D, c["wo1"]],
                                         start=True, stop=True)
                    last.then_inc(W_mm, 1)

                over_tiles(pe, project)

            @block.vector
            def _(dve):
                def residual(g, k):
                    dve.wait_ge(W_mm, g + 1)
                    xt, ht = (a[:, bass.ds(g * T, T), :].rearrange("b t d -> b (t d)") for a in (x, h))
                    dve.tensor_tensor(xt, xt, psW[k][:, 0:T * D], ALU.add).then_inc(x_set, 1)
                    dve.wait_ge(x_set, g + 1)
                    dve.tensor_tensor(ht, ht, xt, ALU.add).then_inc(h_set, 1)

                over_tiles(dve, residual)


def program(nc, x, early_d, late_d, out, phases=99):
    with ExitStack() as ctx:
        def sb(name, shape, dt=F32):
            return ctx.enter_context(nc.sbuf_tensor(name, shape, dt))
        early = sb("early", [128, columns(EARLY)[1]])
        late = sb("late", [128, columns(LATE)[1]])
        h = sb("h", [B, L, D])
        n_all = sb("n_all", [B, L, D])
        minus_half = sb("minus_half", [B, T])
        tokenizer(nc, x, early_d, late_d, early, late, h, minus_half)
        if phases > 1:
            attention0(nc, early, h, n_all, minus_half)
        if phases > 2:
            moe(nc, 0, late, early, h, h, None, minus_half)
        if phases > 3:
            recurrence(nc, late, early, h, minus_half)
        if phases > 4:
            attention1(nc, late, early, h, n_all, minus_half)
        if phases > 5:
            moe(nc, 1, late, early, n_all, h, out, minus_half)



def resize_matrix(n):
    scale = n / GRID
    at = (np.arange(GRID) + 0.5) * scale - 0.5
    w = np.maximum(0.0, 1.0 - np.abs(at[:, None] - np.arange(n)[None, :]) / scale)
    return w / w.sum(axis=1, keepdims=True)


def haar(n):
    lo, hi = np.zeros((n // 2, n)), np.zeros((n // 2, n))
    for k in range(n // 2):
        lo[k, 2 * k], lo[k, 2 * k + 1] = 1, 1
        hi[k, 2 * k], hi[k, 2 * k + 1] = 1, -1
    return lo * 0.5 ** 0.5, hi * 0.5 ** 0.5


MAPS = [(0, 0), (1, 0), (0, 1), (1, 1), (3, 2), (2, 3), (3, 3)]


def shape_constants():
    lo1, hi1 = haar(IMG)
    lo2, hi2 = haar(IMG // 2)
    m1, m2 = resize_matrix(IMG // 2), resize_matrix(IMG // 4)
    rows = np.concatenate([m2 @ lo2 @ lo1, m2 @ hi2 @ lo1, m1 @ lo1, m1 @ hi1])
    t = np.arange(L)
    is_cos = (np.arange(128) % 64 < 32)[:, None]
    top = (np.arange(128) < 64)[:, None]
    row = np.arange(128)
    s, q = np.meshgrid(t, t, indexing="ij")
    inv = 1.0 / 10000.0 ** (np.arange(0, HD, 2, dtype=np.float32) / HD)
    emb = np.outer(t.astype(np.float32), inv.astype(np.float32))
    emb = np.concatenate([emb, emb], axis=1).T
    swap_sign = np.where(np.arange(HD) < HD // 2, -1.0, 1.0)[:, None]
    rope = np.tile(np.concatenate([np.cos(emb), np.sin(emb) * swap_sign]), (NH, 1))
    J = np.zeros((128, 128))
    J[row[64:], row[:64]], J[row[:64], row[64:]] = -1, 1
    return {
        "rowsT": rows.T, "ident": np.eye(128), "stack2": np.concatenate([np.eye(64)] * 2),
        "quarter": np.where(top, 0.25, 0.0), "half_pi": np.where(top, PI / 2, 0.0),
        "feat_sign": np.where(is_cos, -1.0, 1.0), "sin_scale": np.where(is_cos, -PI_BELOW, PI_BELOW),
        "sin_bias": np.where(is_cos, PI / 2, 0.0),
        "causal0": np.where(s <= q, 1 / np.sqrt(32.0 * (q + 1)), 0.0),
        "pos_norm": np.tile(1 / np.sqrt(t + 1.0), (128, 1)),
        "descend": np.tile(np.arange(E, 0, -1.0), (128, T)),
        "c_sign": np.where(top, 1.0, -1.0), "rotJ": J,
        "fold": (row[:, None] // 32 == row[None] // 32) & (row[:, None] % HD == row[None] % HD),
        "ropeq": rope / 4, "ropek": rope,
        "mask1": np.where(s <= q, 0.0, -1e30).T,
    }


def packed(widths, parts):
    cols, total = columns(widths)
    out = np.zeros((128, total), np.float32)
    for name, at in cols.items():
        a = np.asarray(parts[name], np.float32)
        out[:a.shape[0], at] = a.reshape(a.shape[0], -1)
    return out


def laid_out(i):
    p = dict(shape_constants())
    row = lambda v: np.asarray(v).reshape(1, -1)
    col = lambda v: np.asarray(v).reshape(-1, 1)
    twice = lambda a: np.concatenate([a, a])
    over = lambda v, n=128: np.broadcast_to(row(v), (n, np.size(v)))
    tokW = np.zeros((4, 4, GRID, GRID, D), np.float32)
    for f, (rk, ck) in enumerate(MAPS):
        for j in range(GRID):
            tokW[rk, ck, j, j] = i["L0_tok_W"][f]
    p["tokW"] = tokW.reshape(128, GRID * D)
    p["tokb"] = over(np.tile(i["L0_tok_b"], GRID))
    p["cls"] = over(i["cls_tok"])
    a = {k[8:]: v for k, v in i.items() if k.startswith("L0_attn_")}
    p["wkq1"] = np.concatenate([np.concatenate([a["Wk1"], a["Wq1"]], 1), row(np.concatenate([a["bk1"], a["bq1"]]))])
    wkq2 = np.zeros((128, 128), np.float32)
    wkq2[:64, 0:32] = wkq2[:64, 32:64] = a["Wk2"]
    wkq2[64:, 64:96] = wkq2[64:, 96:128] = a["Wq2"]
    p["wkq2"] = wkq2
    p["bkq2"] = col(np.concatenate([a["bk2"], a["bk2"], a["bq2"], a["bq2"]]))
    p["wg1"] = np.concatenate([a["Wg1"], row(a["bg1"])])
    p["wg2"] = np.concatenate([a["Wg2"], row(a["bg2"])])
    p["wvc"] = np.concatenate([a["Wvc"], row(a["bvc"])])
    wvp = np.concatenate([a["Wvp"], row(a["bvp"])])
    p["wvp"] = np.concatenate([wvp, wvp], 1)
    p["phase"] = twice(a["base_phases"][:L].T)
    p["wo0"] = np.concatenate([a["Wo"], row(a["bo"])])
    p["lng"], p["lnb"] = col(a["ln_g"]), col(a["ln_b"])
    p["up0"] = twice(i["L0_ffn_W1"].reshape(-1, D).T)
    p["down0"] = i["L0_ffn_W2"].transpose(2, 0, 1).reshape(2, SPLIT, E, D).transpose(1, 2, 0, 3)
    p["gate0"] = twice(i["L0_ffn_Wg"].T)
    p["gbias0"] = over(i["L0_ffn_bg"])
    p["b1"] = i["L0_ffn_b1"].reshape(CH0, SPLIT).T
    p["b2"] = i["L0_ffn_b2"].reshape(E // 2, 2 * D).T
    r = {k[8:]: v for k, v in i.items() if k.startswith("L1_attn_")}
    p["bT"] = np.concatenate([r["B_re"].T, r["B_im"].T], 1)
    p["gamma"] = over(np.tile(r["gamma_log"], 2), 64)
    p["nu"], p["theta"] = twice(col(r["nu_log"])), twice(col(r["theta_log"]))
    p["cT"] = np.concatenate([r["C_re"].T, r["C_im"].T])
    f = {k[7:]: v for k, v in i.items() if k.startswith("L1_ffn_")}
    swap = (np.arange(HD) + HD // 2) % HD
    for name, w, per in (("wqx", f["wq"], 1), ("wkx", f["wk"], 2)):
        cols = []
        for hd in range(NH):
            own = w[(hd // per) * HD:(hd // per + 1) * HD]
            cols += [own, own[swap]]
        p[name] = np.concatenate(cols).T
    p["wv"], p["wo1"] = f["wv"].T, f["wo"].T
    p["ln1"], p["ln2"] = twice(col(f["ln1_w"])), over(f["ln2_w"])
    p["gate1"] = twice(f["router_w"].T)
    ups, downs = np.zeros((2, E // 2, 3, SPLIT, D), np.float32), np.zeros((E // 2, 4, SPLIT, D), np.float32)
    for pair in range(E // 2):
        for side in range(2):
            e = 2 * pair + side
            for kind, w in enumerate((f["w1"], f["w3"])):
                ups[kind, pair, side] = w[e, :SPLIT]
                ups[kind, pair, 2, 64 * side:64 * side + REST1] = w[e, SPLIT:]
            downs[pair, side] = f["w2"][e, :, :SPLIT].T
            downs[pair, 2 + side, 64 * side:64 * side + REST1] = f["w2"][e, :, SPLIT:].T
    p["up1"] = twice(ups.reshape(-1, D).T)
    p["down1"] = downs.reshape(2 * E, SPLIT, D).transpose(1, 0, 2)
    return {"x": np.ascontiguousarray(i["x"][:, 0].transpose(1, 0, 2)),
            "early": packed(EARLY, p), "late": packed(LATE, p)}


def kernel(**inputs):
    import concourse.bacc as bacc
    from concourse.bass_utils import run_bass_kernel_spmd

    arrays = laid_out({k: np.asarray(v) for k, v in inputs.items()})
    nc = bacc.Bacc("TRN2", target_bir_lowering=False, num_devices=1)
    args = [nc.dram_tensor(f"in_{k}", a.shape, F32, kind="ExternalInput").ap() for k, a in arrays.items()]
    out = nc.dram_tensor("out_tokens", (B, L, D), F32, kind="ExternalOutput").ap()
    program(nc, *args, out)
    r = run_bass_kernel_spmd(nc, [{f"in_{k}": a for k, a in arrays.items()}], core_ids=[0])
    return r.results[0]["out_tokens"]
```
